# Optimizing a Trainium2 kernel written in Bass

```python
import numpy as np
import jax
import jax.numpy as jnp

def _softmax(x, axis=-1):
    return jax.nn.softmax(x, axis=axis)

def _gelu(x):
    return jax.nn.gelu(x, approximate=True)

def _silu(x):
    return jax.nn.silu(x)

def _sigmoid(x):
    return jax.nn.sigmoid(x)

def _layernorm(x, axis=-1, eps=1e-05):
    m = jnp.mean(x, axis=axis, keepdims=True)
    v = jnp.var(x, axis=axis, keepdims=True)
    return (x - m) / jnp.sqrt(v + eps)

def _scatter_add(tgt, idx, src, axis=0):
    return tgt.at[idx].add(src)

def _segment_sum(src, seg, n):
    return jax.ops.segment_sum(src, seg, n)
kernel_name = 'mk_xattn_ffn_d2_seqx_r2_6b9350'

def setup_inputs(seed: int=0):
    np.random.seed(seed)
    _w = jnp.asarray

    def _rec_inputs():
        import jax
        import jax.numpy as jnp
        _rk = jax.random.key(seed)
        x = -0.0003929 + 0.9999 * jax.random.normal(jax.random.fold_in(_rk, 1), (8, 512, 2048), jnp.float32)
        _lenS = 512 - jax.random.randint(jax.random.fold_in(_rk, 7), (8,), 0, max(1, 512 // 4) + 1, jnp.int32)
        _lenS2 = 512 - jax.random.randint(jax.random.fold_in(_rk, 8), (8,), 0, max(1, 512 // 4) + 1, jnp.int32)
        _ctx_4096P = jax.random.normal(jax.random.fold_in(_rk, 11), (8, 16, 2048), jnp.float32)
        _ctx_4096c = jax.random.dirichlet(jax.random.fold_in(_rk, 511), 0.3 * jnp.ones((16,), jnp.float32), (8, 512))
        _ctx_4096t = jnp.einsum('bsk,bkd->bsd', _ctx_4096c, _ctx_4096P)
        _ctx_4096t = _ctx_4096t * jax.lax.rsqrt(jnp.mean(jnp.square(_ctx_4096t)) + 1e-12) * 0.953939
        ctx_4096 = 2.81802e-05 + 1.00001 * (_ctx_4096t + 0.3 * jax.random.normal(jax.random.fold_in(_rk, 611), (8, 512, 2048), jnp.float32))
        return (x, ctx_4096)
    x, ctx_4096 = _rec_inputs()

    def _L0_xattn_setup():
        import jax, jax.numpy as jnp
        import numpy as np
        EMB_DIM = 256
        HEADS = 8
        key = jax.random.key(seed)
        kq, kk, kv = jax.random.split(key, 3)
        B, C, N = (8, EMB_DIM, 2048)
        q = jax.random.normal(kq, (B, C, N), dtype=jnp.float32)
        k = jax.random.normal(kk, (B, C, N), dtype=jnp.float32)
        v = jax.random.normal(kv, (B, C, N), dtype=jnp.float32)
        return {'q': q, 'k': k, 'v': v}
    _L0_xattn_all = _L0_xattn_setup()
    _L0_xattn_in = {k: v for k, v in _L0_xattn_all.items() if k in ()}
    del _L0_xattn_all

    def _L0_ffn_setup():
        import jax, jax.numpy as jnp
        import numpy as np
        R = 16
        LORA_ALPHA = 16
        SCALING = LORA_ALPHA / R
        key = jax.random.key(seed)
        kx, kr, ka = jax.random.split(key, 3)
        B, S, D, DO, E = (4, 1024, 2048, 2048, 8)
        x = jax.random.normal(kx, (B, S, D), dtype=jnp.float32)
        bound_r = 1.0 / np.sqrt(D)
        route_w = jax.random.uniform(kr, (E, D), jnp.float32, -bound_r, bound_r)
        bound_a = 1.0 / np.sqrt(D)
        A = jax.random.uniform(ka, (E, R, D), jnp.float32, -bound_a, bound_a)
        kb = jax.random.fold_in(key, 7)
        Bw = jax.random.normal(kb, (E, DO, R), dtype=jnp.float32) * 0.02
        return {'x': x, 'route_w': route_w, 'A': A, 'Bw': Bw}
    _L0_ffn_all = _L0_ffn_setup()
    _L0_ffn_in = {k: v for k, v in _L0_ffn_all.items() if k in ('route_w', 'A', 'Bw')}
    del _L0_ffn_all

    def _L1_xattn_setup():
        import jax, jax.numpy as jnp
        import numpy as np
        key = jax.random.key(seed)
        k1, k2 = jax.random.split(key)
        B, Lq, Lk, D = (16, 512, 1024, 2048)
        query = jax.random.normal(k1, (B, Lq, D), dtype=jnp.float32)
        key_t = jax.random.normal(k2, (B, Lk, D), dtype=jnp.float32)
        return {'query': query, 'key': key_t}
    _L1_xattn_all = _L1_xattn_setup()
    _L1_xattn_in = {k: v for k, v in _L1_xattn_all.items() if k in ()}
    del _L1_xattn_all

    def _L1_ffn_setup():
        import jax, jax.numpy as jnp
        import numpy as np
        RANKS = (8, 16, 32, 64)
        TOPK = 1
        SCALING = 1.0 / 4
        key = jax.random.key(seed)
        ks = jax.random.split(key, 7)
        D_IN, D_OUT, MAX_R, N_RANKS = (2048, 2048, 64, len(RANKS))
        B_, S_ = (4, 1024)
        return {'hidden_states': jax.random.normal(ks[0], (B_, S_, D_IN), jnp.float32), 'W': jax.random.normal(ks[1], (D_OUT, D_IN), jnp.float32) * 0.02, 'b': jax.random.normal(ks[2], (D_OUT,), jnp.float32) * 0.02, 'A': jax.random.normal(ks[3], (MAX_R, D_IN), jnp.float32) * 0.02, 'B': jnp.zeros((D_OUT, MAX_R), jnp.float32) + jax.random.normal(ks[4], (D_OUT, MAX_R), jnp.float32) * 0.02, 'gate_w': jax.random.normal(ks[5], (N_RANKS, D_IN), jnp.float32) * 0.02, 'gate_b': jax.random.normal(ks[6], (N_RANKS,), jnp.float32) * 0.02}
    _L1_ffn_all = _L1_ffn_setup()
    _L1_ffn_in = {k: v for k, v in _L1_ffn_all.items() if k in ('W', 'b', 'A', 'B', 'gate_w', 'gate_b')}
    del _L1_ffn_all
    return {'x': x, 'ctx_4096': ctx_4096, 'L0_ffn_route_w': _L0_ffn_in['route_w'], 'L0_ffn_A': _L0_ffn_in['A'], 'L0_ffn_Bw': _L0_ffn_in['Bw'], 'L1_ffn_W': _L1_ffn_in['W'], 'L1_ffn_b': _L1_ffn_in['b'], 'L1_ffn_A': _L1_ffn_in['A'], 'L1_ffn_B': _L1_ffn_in['B'], 'L1_ffn_gate_w': _L1_ffn_in['gate_w'], 'L1_ffn_gate_b': _L1_ffn_in['gate_b']}

def reference(x, ctx_4096, L0_ffn_route_w, L0_ffn_A, L0_ffn_Bw, L1_ffn_W, L1_ffn_b, L1_ffn_A, L1_ffn_B, L1_ffn_gate_w, L1_ffn_gate_b):
    import jax
    import jax.numpy as jnp

    def _L0_xattn_ref(q, k, v):
        import jax, jax.numpy as jnp
        import numpy as np
        EMB_DIM = 256
        HEADS = 8
        B, C, N = q.shape
        H = HEADS
        dh = C // H
        qh = q.transpose(0, 2, 1).reshape(B, N, H, dh)
        kh = k.transpose(0, 2, 1).reshape(B, N, H, dh)
        vh = v.transpose(0, 2, 1).reshape(B, N, H, dh)
        qh = jax.nn.softmax(qh, axis=3)
        kh = jax.nn.softmax(kh, axis=1)
        kvs = jnp.einsum('bnhd,bnhe->bhde', kh, vh)
        out = jnp.einsum('bnhd,bhde->bnhe', qh, kvs)
        return out.transpose(0, 2, 3, 1).reshape(B, C, N)

    def _L0_ffn_ref(x, route_w, A, Bw):
        import jax, jax.numpy as jnp
        import numpy as np
        R = 16
        LORA_ALPHA = 16
        SCALING = LORA_ALPHA / R
        logits = jnp.einsum('bsd,ed->bse', x, route_w)
        topk_v, topk_idx = jax.lax.top_k(logits, 1)
        E = logits.shape[-1]
        route_weight = jax.nn.one_hot(topk_idx[..., 0], E, dtype=logits.dtype) * topk_v
        h = jnp.einsum('bsd,erd->bser', x, A)
        wh = route_weight[..., None] * h
        out = jnp.einsum('bser,eor->bso', wh, Bw) * SCALING
        return out

    def _L1_xattn_ref(query, key):
        import jax, jax.numpy as jnp
        import numpy as np
        a = jnp.einsum('bqd,bkd->bqk', query, key)
        e = jax.nn.softmax(a, axis=-1)
        c = jnp.einsum('bqk,bkd->bqd', e, key)
        return c

    def _L1_ffn_ref(hidden_states, W, b, A, B, gate_w, gate_b):
        import jax, jax.numpy as jnp
        import numpy as np
        RANKS = (8, 16, 32, 64)
        TOPK = 1
        SCALING = 1.0 / 4
        bsz, seq, d_in = hidden_states.shape
        out = jnp.einsum('bsd,od->bso', hidden_states, W) + b
        x = hidden_states.reshape(-1, d_in)
        scores = x @ gate_w.T + gate_b
        probs = jax.nn.softmax(scores, axis=-1)
        routing_weights, selected = jax.lax.top_k(probs, TOPK)
        routing_weights = routing_weights / jnp.sum(routing_weights, axis=-1, keepdims=True)
        lora_outputs = jnp.stack([x @ A[:r, :].T @ B[:, :r].T for r in RANKS], axis=1)
        sel = jnp.take_along_axis(lora_outputs, selected[:, :, None], axis=1)
        final = jnp.sum(sel * routing_weights[:, :, None], axis=1)
        return out + final.reshape(bsz, seq, -1)
    x = x + _L0_xattn_ref(_layernorm(x, axis=-1), ctx_4096, ctx_4096)
    x = x + _L0_ffn_ref(_layernorm(x, axis=-1), L0_ffn_route_w, L0_ffn_A, L0_ffn_Bw)
    x = x + _L1_xattn_ref(_layernorm(x, axis=-1), ctx_4096)
    x = x + _L1_ffn_ref(_layernorm(x, axis=-1), L1_ffn_W, L1_ffn_b, L1_ffn_A, L1_ffn_B, L1_ffn_gate_w, L1_ffn_gate_b)
    return x

_drawn_inputs = setup_inputs


def setup_inputs(seed=0):
    import zlib

    import numpy as np

    out = dict(_drawn_inputs(seed))
    spreads = {}
    factors = {'L1_ffn_b': 5.379, 'L1_ffn_gate_b': 35.16}
    for name, (base, spread) in spreads.items():
        noise = np.random.default_rng([zlib.crc32(name.encode()), seed]).standard_normal(out[name].shape)
        drawn = base * np.exp(spread * noise) if base else spread * noise
        out[name] = jnp.asarray(drawn.astype(out[name].dtype))
    for name, factor in factors.items():
        out[name] = (out[name] * factor).astype(out[name].dtype)
    return out
```

```python
from contextlib import ExitStack

import concourse.bass as bass
from concourse import mybir

F32 = mybir.dt.float32
F16 = mybir.dt.float16
U32 = mybir.dt.uint32
ALU = mybir.AluOpType
ACT = mybir.ActivationFunctionType
AX_X = mybir.AxisListType.X

P = 128
D = 2048
DC = D // P
ROWS = 512
TPB = ROWS // P
HD = 64
Q = 512
NQ = D // Q
E = 8
R = 16
ER = E * R
EPS = 1e-5
RING = 4
NUM = 2 * HD + 2
NUM_FILLS = [3, 3, 3, 3, 3, 1]
MAXR = 64
NG = 4
RANKS = (8, 16, 32, 64)
AG = MAXR + NG
XS = 64.0
TOP = 4096.0


class Slot:

    def __init__(self, n, rounds=0):
        self.n, self.rounds = n, rounds

    def back(self, k):
        return Slot(self.n - k, self.rounds)


class Counted:

    def __init__(self, sem, stages, tiles, slots_per_round, first):
        self.sem, self.stages, self.tiles, self.first = sem, stages, tiles, first
        self.per_round = slots_per_round * sum(k for _, k, _ in stages)

    def _count(self, slot, stage, k):
        total = 0
        for s in range(self.first, slot.n + 1):
            for name, raises, offset in self.stages:
                if s == slot.n and name == stage:
                    total += k
                    return total + slot.rounds * self.per_round
                if 0 <= s + offset < self.tiles:
                    total += raises
        raise KeyError(stage)

    def before(self, stage, slot):
        return self._count(slot, stage, 0)

    def after(self, stage, slot, k=None):
        if k is None:
            k = next(r for name, r, _ in self.stages if name == stage)
        return self._count(slot, stage, k)


def wait(eng, sem, value):
    if isinstance(value, int) and value <= 0:
        return
    eng.wait_ge(sem, value)


def pass_a(nc, ctx, x, c_rows, c_cols, ra, bwt, x3):
    batches = x.shape[0] // ROWS
    tiles = batches * TPB
    per_round = 2 * TPB
    first = -2

    def sb(name, shape, dt=F32):
        return ctx.enter_context(nc.sbuf_tensor(name, shape, dt))

    def sem(name):
        return ctx.enter_context(nc.semaphore(name))

    ctxT = sb("ctxT", [P, 2, DC, ROWS])
    ctxN = sb("ctxN", [P, TPB, D])
    xt = sb("xt", [P, TPB, D])
    crow = sb("crow", [P, D])
    expT = sb("expT", [P, DC, P])
    work_a = sb("work_a", [P, DC, P])
    work_b = sb("work_b", [P, D])
    ln2T = sb("ln2T", [P, DC, P])
    ln3T = sb("ln3T", [P, DC, P])
    ra_sb = sb("ra_sb", [P, DC, E + ER])
    bwt_sb = sb("bwt_sb", [ER, D])
    kv = sb("kv", [P, 2, NUM])
    prob = sb("prob", [P, ROWS])
    probT = sb("probT", [P, TPB, P])
    wh = sb("wh", [P, ER])
    whT = sb("whT", [ER, P])
    hs = sb("hs", [P, E + ER])
    ident = sb("ident", [P, P])
    order8 = sb("order8", [P, E])
    consts = sb("consts", [P, 3])
    st6 = sb("st6", [P, 3, NQ, 6])
    mv = sb("mv", [P, 3, 2])
    veps = sb("veps", [P, 3])
    rstd = sb("rstd", [P, 3])
    shift1 = sb("shift1", [P, 3])
    shift = sb("shift", [P, 3])
    fence = sb("fence", [P, 1])
    rden = sb("rden", [P, DC, 2])
    route = sb("route", [P, 4, E])
    ncmax = sb("ncmax", [P, 1])
    csum = sb("csum", [P, 2])
    rcsum = sb("rcsum", [P, 1])
    nsmax = sb("nsmax", [P, 1])
    psum_row = sb("psum_row", [P, 1])
    rprob = sb("rprob", [P, 1])
    tb = [ctx.enter_context(nc.psum_tensor(f"tb{k}", [P, Q], F32)) for k in range(RING)]
    wb = [ctx.enter_context(nc.psum_tensor(f"wb{k}", [P, Q], F32)) for k in range(RING)]

    def counted(name, stages):
        return Counted(sem(name), stages, tiles, per_round, first)

    T_STAGES = [("expT", 4, 1), ("scores", 1, -2), ("whT", 1, -1), ("probT", 1, -2), ("ln2T", 4, 0), ("ln3T", 4, -1)]
    W_STAGES = [("down", 1, -1), ("num", 6, 0), ("attn1", 4, 0), ("kvs", 1, 1), ("up", 4, -1), ("pv", 4, -2)]
    t_filled = counted("t_filled", T_STAGES)
    t_drained = counted("t_drained", T_STAGES)
    w_filled = counted("w_filled", W_STAGES)
    w_drained = counted("w_drained", W_STAGES)
    steps = counted("steps", [("down", 4, -1), ("num", 6, 0), ("attn1", 4, 0), ("kvs", 1, 1), ("up", 4, -1), ("ln1", 4, 1), ("pv", 1, -2)])
    stats_ready = counted("stats_ready", [("attn1", 1, 0), ("up", 1, -1), ("ln1", 1, 1)])
    pool_steps = counted("pool_steps", [("attn1", 2, 0), ("up", 2, -1), ("ln1", 2, 1)])
    rstd_ready = counted("rstd_ready", [("attn1", 1, 0), ("up", 1, -1), ("ln1", 1, 1)])
    wh_ready = counted("wh_ready", [("down", 1, -1)])
    smax_ready = counted("smax_ready", [("scores", 1, -2)])
    cmax_ready = counted("cmax_ready", [("cexp", 1, 2)])
    cexp_ready = counted("cexp_ready", [("cexp", 1, 2)])
    q_ready = counted("q_ready", [("q", 1, 1)])
    ln2_ready = counted("ln2_ready", [("ln2", 1, 0)])
    ln3_ready = counted("ln3_ready", [("ln3", 1, -1)])
    c_loaded = counted("c_loaded", [("load", 16, 2)])
    x_loaded = [sem(f"x_loaded{j}") for j in range(TPB)]
    x_stored = [sem(f"x_stored{j}") for j in range(TPB)]
    t_loaded = [sem(f"t_loaded{j}") for j in range(NQ)]
    n_loaded = [sem(f"n_loaded{j}") for j in range(NQ)]
    const_loaded = sem("const_loaded")
    const_ready = sem("const_ready")
    ident_blank = sem("ident_blank")
    kv_blank = sem("kv_blank")

    LN1, LN2, LN3 = 0, 1, 2

    def batch(slot, offset):
        return (slot.n + offset) // TPB + 2 * slot.rounds, (slot.n + offset) % TPB

    def here(slot, offset):
        return 0 <= slot.n + offset < tiles

    with nc.Block() as block:

        @block.sync
        def _(sp):
            sp.dma_start(ra_sb[:], ra).then_inc(const_loaded, 16)
            sp.dma_start(bwt_sb[:], bwt).then_inc(const_loaded, 16)

            def load_cols(b, parity):
                for k in range(NQ):
                    sp.dma_start(ctxT[:, parity, k * 4:k * 4 + 4, :], c_cols[bass.ds(b * P, P), k * 4:k * 4 + 4, :]
                                 ).then_inc(t_loaded[k], 16)

            def load_x(b, j):
                sp.dma_start(xt[:, j, :], x[bass.ds(b * ROWS + j * P, P), :]).then_inc(x_loaded[j], 16)

            def stages(slot):
                if here(slot, 2):
                    b, j = batch(slot, 2)
                    if here(slot, 1):
                        wait(sp, t_drained.sem, t_drained.after("expT", slot))
                    sp.dma_start(crow[:], c_rows[bass.ds(b * ROWS + j * P, P), :]).then_inc(c_loaded.sem, 16)
                if slot.n == first:
                    load_x(0, 0)
                    load_cols(0, 0)
                    for k in range(NQ):
                        sp.dma_start(ctxN[:, :, k * Q:(k + 1) * Q],
                                     c_rows[0:ROWS, k * Q:(k + 1) * Q].rearrange("(a p) n -> p a n", p=P)
                                     ).then_inc(n_loaded[k], 16)
                if slot.n == 0:
                    load_cols(1, 1)
                b, j = batch(slot, 0)
                if slot.n >= TPB and j == 1 and here(slot, 0):
                    for k in range(NQ):
                        wait(sp, w_filled.sem, w_filled.after("pv", slot, k + 1))
                        sp.dma_start(ctxN[:, :, k * Q:(k + 1) * Q],
                                     c_rows[bass.ds(b * ROWS, ROWS), k * Q:(k + 1) * Q].rearrange("(a p) n -> p a n", p=P)
                                     ).then_inc(n_loaded[k], 16)
                if here(slot, -2):
                    bs, js = batch(slot, -2)
                    wait(sp, w_drained.sem, w_drained.after("pv", slot))
                    sp.dma_start(x3[bass.ds(bs * ROWS + js * P, P), :], xt[:, js, :]).then_inc(x_stored[js], 16)
                if slot.n >= TPB and j == 1 and here(slot, TPB):
                    wait(sp, t_filled.sem, t_filled.after("scores", slot))
                    load_cols(b + 1, (slot.n // TPB + 1) % 2)
                if slot.n > first and here(slot, 2):
                    bl, jl = batch(slot, 2)
                    if here(slot, -2):
                        sp.wait_ge(x_stored[jl], bl * 16)
                    load_x(bl, jl)

            for s in range(first, TPB):
                stages(Slot(s))
            with sp.Fori(0, (batches - 2) // 2) as r:
                for s in range(TPB, 3 * TPB):
                    stages(Slot(s, r))
            for s in range(tiles - TPB, tiles + 2):
                stages(Slot(s))
            for j in range(TPB):
                sp.wait_ge(x_stored[j], batches * 16)

        @block.gpsimd
        def _(pool):
            nc.gpsimd.memset(ident[:], 0.0).then_inc(ident_blank, 1)
            for n, value in enumerate((EPS, -0.5, -1.0)):
                nc.gpsimd.memset(consts[:, n:n + 1], value)
            for e in range(E):
                nc.gpsimd.memset(order8[:, e:e + 1], float(E - e))
            pool.wait_ge(ident_blank, 1)
            nc.gpsimd.affine_select(out=ident[:], in_=ident[:], compare_op=ALU.not_equal, fill=1.0, base=0,
                                    pattern=[[-1, P]], channel_multiplier=1).then_inc(const_ready, 1)

            def layernorm_scale(slot, stage, which):
                base = pool_steps.before(stage, slot)
                one = slice(which, which + 1)
                pool.wait_ge(stats_ready.sem, stats_ready.after(stage, slot))
                nc.gpsimd.tensor_tensor(shift1[:, one], mv[:, which, 0:1], consts[:, 2:3], ALU.mult)
                nc.gpsimd.tensor_tensor(veps[:, one], mv[:, which, 1:2], consts[:, 0:1], ALU.add
                                        ).then_inc(pool_steps.sem, 1)
                pool.wait_ge(pool_steps.sem, base + 1)
                nc.gpsimd.tensor_tensor(rstd[:, one], veps[:, one], consts[:, 1:2], ALU.pow
                                        ).then_inc(pool_steps.sem, 1)
                pool.wait_ge(pool_steps.sem, base + 2)
                nc.gpsimd.tensor_tensor(shift[:, one], shift1[:, one], rstd[:, one], ALU.mult
                                        ).then_inc(rstd_ready.sem, 1)

            def stages(slot):
                if here(slot, 0):
                    layernorm_scale(slot, "attn1", LN2)
                if here(slot, -1):
                    layernorm_scale(slot, "up", LN3)
                if here(slot, 1):
                    layernorm_scale(slot, "ln1", LN1)

            for s in range(first, TPB):
                stages(Slot(s))
            with pool.Fori(0, (batches - 2) // 2) as r:
                for s in range(TPB, 3 * TPB):
                    stages(Slot(s, r))
            for s in range(tiles - TPB, tiles + 2):
                stages(Slot(s))

        @block.scalar
        def _(act):
            def bank(stage, slot, k):
                return tb[t_filled.after(stage, Slot(slot.n), k) % RING]

            def drain(stage, slot, dst):
                for k in range(4):
                    act.wait_ge(t_filled.sem, t_filled.after(stage, slot, k + 1))
                    nc.scalar.activation(dst[:, 4 * k:4 * k + 4, :].rearrange("p a b -> p (a b)"),
                                         bank(stage, slot, k)[:], ACT.Copy
                                         ).then_inc(t_drained.sem, 1)

            def stages(slot):
                if here(slot, 1):
                    drain("expT", slot, expT)
                if here(slot, -2):
                    act.wait_ge(smax_ready.sem, smax_ready.after("scores", slot))
                    nc.scalar.activation(prob[:], bank("scores", slot, 0)[:], ACT.Exp, bias=nsmax[:],
                                         accum_out=psum_row[:]).then_inc(t_drained.sem, 1)
                if here(slot, -1):
                    act.wait_ge(t_filled.sem, t_filled.after("whT", slot))
                    nc.scalar.activation(whT[:], bank("whT", slot, 0)[:, 0:P], ACT.Copy).then_inc(t_drained.sem, 1)
                if here(slot, -2):
                    act.wait_ge(t_filled.sem, t_filled.after("probT", slot))
                    nc.scalar.activation(probT[:].rearrange("p a b -> p (a b)"), bank("probT", slot, 0)[:], ACT.Copy).then_inc(t_drained.sem, 1)
                if here(slot, 2):
                    p = (slot.n + 2) % 2
                    act.wait_ge(cmax_ready.sem, cmax_ready.after("cexp", slot))
                    nc.scalar.activation(crow[:], crow[:], ACT.Exp, bias=ncmax[:], accum_out=csum[:, p:p + 1]
                                         ).then_inc(cexp_ready.sem, 1)
                if here(slot, 0):
                    act.wait_ge(rstd_ready.sem, rstd_ready.after("attn1", slot))
                    nc.scalar.activation(work_a[:].rearrange("p a b -> p (a b)"), xt[:, slot.n % TPB, :], ACT.Identity,
                                         scale=rstd[:, LN2:LN2 + 1], bias=shift[:, LN2:LN2 + 1]
                                         ).then_inc(ln2_ready.sem, 1)
                if here(slot, -1):
                    act.wait_ge(rstd_ready.sem, rstd_ready.after("up", slot))
                    nc.scalar.activation(work_b[:], xt[:, (slot.n - 1) % TPB, :], ACT.Identity,
                                         scale=rstd[:, LN3:LN3 + 1], bias=shift[:, LN3:LN3 + 1]
                                         ).then_inc(ln3_ready.sem, 1)
                if here(slot, 0):
                    drain("ln2T", slot, ln2T)
                if here(slot, -1):
                    drain("ln3T", slot, ln3T)
                if here(slot, 1):
                    act.wait_ge(rstd_ready.sem, rstd_ready.after("ln1", slot))
                    nc.scalar.activation(work_b[:], xt[:, (slot.n + 1) % TPB, :], ACT.Exp,
                                         scale=rstd[:, LN1:LN1 + 1], bias=shift[:, LN1:LN1 + 1]
                                         ).then_inc(q_ready.sem, 1)

            for s in range(first, TPB):
                stages(Slot(s))
            with act.Fori(0, (batches - 2) // 2) as r:
                for s in range(TPB, 3 * TPB):
                    stages(Slot(s, r))
            for s in range(tiles - TPB, tiles + 2):
                stages(Slot(s))

        @block.vector
        def _(dve):
            def bank(stage, slot, k):
                return wb[w_filled.after(stage, Slot(slot.n), k) % RING]

            def filled(stage, slot, k):
                dve.wait_ge(w_filled.sem, w_filled.after(stage, slot, k))

            def add_and_stats(slot, stage, offset, which):
                xr = xt[:, (slot.n + offset) % TPB, :]
                base = steps.before(stage, slot)
                for k in range(NQ):
                    part = xr[:, k * Q:(k + 1) * Q]
                    filled(stage, slot, k + 1)
                    nc.vector.tensor_tensor(part, bank(stage, slot, k)[:], part, ALU.add).then_inc(w_drained.sem, 1)
                    dve.wait_ge(w_drained.sem, w_drained.after(stage, slot, k + 1))
                    nc.vector.bn_stats(st6[:, which, k, :], part).then_inc(steps.sem, 1)
                dve.wait_ge(steps.sem, base + NQ)
                nc.vector.memset(fence[:], 0.0)
                nc.vector.bn_aggr(mv[:, which, :], st6[:, which, :, :]).then_inc(stats_ready.sem, 1)

            def stages(slot):
                if here(slot, -1):
                    base = steps.before("down", slot)
                    filled("down", slot, 1)
                    nc.vector.tensor_copy(hs[:], bank("down", slot, 0)[:, 0:E + ER]).then_inc(w_drained.sem, 1)
                    dve.wait_ge(w_drained.sem, w_drained.after("down", slot))
                    nc.vector.tensor_reduce(route[:, 0, 0:1], hs[:, 0:E], AX_X, ALU.max).then_inc(steps.sem, 1)
                    dve.wait_ge(steps.sem, base + 1)
                    nc.vector.scalar_tensor_tensor(route[:, 1, :], hs[:, 0:E], route[:, 0, 0:1], order8[:],
                                                   ALU.is_equal, ALU.mult).then_inc(steps.sem, 1)
                    dve.wait_ge(steps.sem, base + 2)
                    nc.vector.tensor_reduce(route[:, 2, 0:1], route[:, 1, :], AX_X, ALU.max).then_inc(steps.sem, 1)
                    dve.wait_ge(steps.sem, base + 3)
                    nc.vector.tensor_scalar(route[:, 3, :], route[:, 1, :], route[:, 2, 0:1], route[:, 0, 0:1],
                                            ALU.is_equal, ALU.mult).then_inc(steps.sem, 1)
                    dve.wait_ge(steps.sem, base + 4)
                    nc.vector.tensor_tensor(wh[:].rearrange("p (e r) -> p e r", e=E),
                                            hs[:, E:].rearrange("p (e r) -> p e r", e=E),
                                            route[:, 3, :].unsqueeze(2).broadcast_to([P, E, R]), ALU.mult
                                            ).then_inc(wh_ready.sem, 1)
                if here(slot, 0):
                    base = steps.before("num", slot)
                    c = 0
                    for k, n in enumerate(NUM_FILLS):
                        filled("num", slot, k + 1)
                        b = bank("num", slot, k)[:, 0:n * NUM].rearrange("p (c m) -> p c m", c=n)
                        nc.vector.reciprocal(rden[:, c:c + n, :], b[:, :, 2 * HD:NUM]).then_inc(steps.sem, 1)
                        dve.wait_ge(steps.sem, base + k + 1)
                        nc.vector.tensor_tensor(work_a[:, c:c + n, :].rearrange("p c (h m) -> p c h m", h=2),
                                                b[:, :, 0:2 * HD].rearrange("p c (h m) -> p c h m", h=2),
                                                rden[:, c:c + n, :].unsqueeze(3).broadcast_to([P, n, 2, HD]),
                                                ALU.mult).then_inc(w_drained.sem, 1)
                        c += n
                if here(slot, -2):
                    dve.wait_ge(t_filled.sem, t_filled.after("scores", slot))
                    b = tb[t_filled.before("scores", Slot(slot.n)) % RING]
                    nc.vector.tensor_reduce(nsmax[:], b[:], AX_X, ALU.max, negate=True).then_inc(smax_ready.sem, 1)
                if here(slot, 0):
                    add_and_stats(slot, "attn1", 0, LN2)
                if here(slot, 1):
                    p = (slot.n + 1) % 2
                    dve.wait_ge(cexp_ready.sem, cexp_ready.after("cexp", slot.back(1)))
                    nc.vector.reciprocal(rcsum[:], csum[:, p:p + 1]).then_inc(steps.sem, 1)
                    dve.wait_ge(steps.sem, steps.after("kvs", slot))
                    filled("kvs", slot, 1)
                    b = bank("kvs", slot, 0)
                    nc.vector.tensor_scalar(kv[0:HD, p, 0:HD], b[0:HD, 0:HD], rcsum[0:HD], None, ALU.mult)
                    nc.vector.tensor_scalar(kv[HD:P, p, HD:2 * HD], b[HD:P, HD:2 * HD], rcsum[HD:P], None, ALU.mult
                                            ).then_inc(w_drained.sem, 1)
                if here(slot, -1):
                    add_and_stats(slot, "up", -1, LN3)
                if here(slot, 2):
                    dve.wait_ge(c_loaded.sem, c_loaded.after("load", slot))
                    nc.vector.tensor_reduce(ncmax[:], crow[:], AX_X, ALU.max, negate=True).then_inc(cmax_ready.sem, 1)
                if here(slot, 1):
                    b1, j1 = batch(slot, 1)
                    base = steps.before("ln1", slot)
                    dve.wait_ge(x_loaded[j1], b1 * 16 + 16)
                    for k in range(NQ):
                        nc.vector.bn_stats(st6[:, LN1, k, :], xt[:, j1, k * Q:(k + 1) * Q]).then_inc(steps.sem, 1)
                    dve.wait_ge(steps.sem, base + NQ)
                    nc.vector.memset(fence[:], 0.0)
                    nc.vector.bn_aggr(mv[:, LN1, :], st6[:, LN1, :, :]).then_inc(stats_ready.sem, 1)
                if here(slot, -2):
                    xr = xt[:, (slot.n - 2) % TPB, :]
                    dve.wait_ge(t_drained.sem, t_drained.after("scores", slot))
                    nc.vector.reciprocal(rprob[:], psum_row[:]).then_inc(steps.sem, 1)
                    dve.wait_ge(steps.sem, steps.after("pv", slot))
                    for k in range(NQ):
                        part = xr[:, k * Q:(k + 1) * Q]
                        filled("pv", slot, k + 1)
                        nc.vector.scalar_tensor_tensor(part, bank("pv", slot, k)[:], rprob[:], part, ALU.mult, ALU.add
                                                       ).then_inc(w_drained.sem, 1)

            nc.vector.memset(kv[:], 0.0).then_inc(kv_blank, 1)
            dve.wait_ge(kv_blank, 1)
            nc.vector.memset(kv[0:HD, :, 2 * HD:2 * HD + 1], 1.0)
            nc.vector.memset(kv[HD:P, :, 2 * HD + 1:NUM], 1.0)
            dve.wait_ge(const_ready, 1)
            for s in range(first, TPB):
                stages(Slot(s))
            with dve.Fori(0, (batches - 2) // 2) as r:
                for s in range(TPB, 3 * TPB):
                    stages(Slot(s, r))
            for s in range(tiles - TPB, tiles + 2):
                stages(Slot(s))

        @block.tensor
        def _(pe):
            pe.wait_ge(const_ready, 1)
            pe.wait_ge(const_loaded, 32)

            def t_bank(stage, slot, k):
                wait(pe, t_drained.sem, t_filled.after(stage, slot, k) - RING + 1)
                return tb[t_filled.after(stage, Slot(slot.n), k) % RING]

            def w_bank(stage, slot, k):
                wait(pe, w_drained.sem, w_filled.after(stage, slot, k) - RING + 1)
                return wb[w_filled.after(stage, Slot(slot.n), k) % RING]

            def transposed(stage, slot, src):
                for k in range(4):
                    b = t_bank(stage, slot, k)
                    for m in range(4):
                        last = nc.tensor.transpose(b[:, m * P:(m + 1) * P], src(4 * k + m), ident[:])
                    last.then_inc(t_filled.sem, 1)

            def stages(slot):
                if here(slot, -1):
                    pe.wait_ge(t_drained.sem, t_drained.after("ln2T", slot.back(1)))
                    b = w_bank("down", slot, 0)
                    for c in range(DC):
                        last = nc.tensor.matmul(b[:, 0:E + ER], ln2T[:, c, :], ra_sb[:, c, :],
                                                start=(c == 0), stop=(c == DC - 1))
                    last.then_inc(w_filled.sem, 1)
                if here(slot, 1):
                    pe.wait_ge(cexp_ready.sem, cexp_ready.after("cexp", slot.back(1)))
                    transposed("expT", slot, lambda c: crow[:, c * P:(c + 1) * P])
                if here(slot, 0):
                    pe.wait_ge(q_ready.sem, q_ready.after("q", slot.back(1)))
                    pe.wait_ge(w_drained.sem, w_drained.after("kvs", slot.back(1)))
                    c = 0
                    for k, n in enumerate(NUM_FILLS):
                        b = w_bank("num", slot, k)
                        for m in range(n):
                            last = nc.tensor.matmul(b[:, m * NUM:(m + 1) * NUM], work_b[:, c * P:(c + 1) * P],
                                                    kv[:, slot.n % 2, :], start=True, stop=True)
                            c += 1
                        last.then_inc(w_filled.sem, 1)
                if here(slot, -2):
                    pe.wait_ge(t_drained.sem, t_drained.after("ln3T", slot.back(1)))
                    b = t_bank("scores", slot, 0)
                    for c in range(DC):
                        last = nc.tensor.matmul(b[:], ln3T[:, c, :], ctxT[:, (slot.n - 2) // TPB % 2, c, :],
                                                start=(c == 0), stop=(c == DC - 1))
                    last.then_inc(t_filled.sem, 1)
                if here(slot, 0):
                    pe.wait_ge(w_drained.sem, w_drained.after("num", slot))
                    for k in range(NQ):
                        b = w_bank("attn1", slot, k)
                        for m in range(4):
                            last = nc.tensor.transpose(b[:, m * P:(m + 1) * P], work_a[:, 4 * k + m, :], ident[:])
                        last.then_inc(w_filled.sem, 1)
                if here(slot, -1):
                    pe.wait_ge(wh_ready.sem, wh_ready.after("down", slot))
                    b = t_bank("whT", slot, 0)
                    nc.tensor.transpose(b[:, 0:P], wh[:], ident[:]).then_inc(t_filled.sem, 1)
                if here(slot, 1):
                    b1, j1 = batch(slot, 1)
                    b = w_bank("kvs", slot, 0)
                    for c in range(DC):
                        if c % 4 == 0:
                            pe.wait_ge(t_drained.sem, t_drained.after("expT", slot, c // 4 + 1))
                            if j1 == 0:
                                pe.wait_ge(t_loaded[c // 4], b1 * 16 + 16)
                        last = nc.tensor.matmul(b[:, 0:P], expT[:, c, :],
                                                ctxT[:, (slot.n + 1) // TPB % 2, c, j1 * P:(j1 + 1) * P],
                                                start=(c == 0), stop=(c == DC - 1))
                    last.then_inc(w_filled.sem, 1)
                if here(slot, -2):
                    pe.wait_ge(t_drained.sem, t_drained.after("scores", slot))
                    b = t_bank("probT", slot, 0)
                    for m in range(TPB):
                        last = nc.tensor.transpose(b[:, m * P:(m + 1) * P], prob[:, m * P:(m + 1) * P], ident[:])
                    last.then_inc(t_filled.sem, 1)
                if here(slot, -1):
                    pe.wait_ge(t_drained.sem, t_drained.after("whT", slot))
                    for k in range(NQ):
                        b = w_bank("up", slot, k)
                        nc.tensor.matmul(b[:], whT[:], bwt_sb[:, k * Q:(k + 1) * Q], start=True, stop=True
                                         ).then_inc(w_filled.sem, 1)
                if here(slot, -2):
                    b2, j2 = batch(slot, -2)
                    pe.wait_ge(t_drained.sem, t_drained.after("probT", slot))
                    for k in range(NQ):
                        if j2 == 0:
                            pe.wait_ge(n_loaded[k], b2 * 16 + 16)
                        b = w_bank("pv", slot, k)
                        for m in range(TPB):
                            last = nc.tensor.matmul(b[:], probT[:, m, :], ctxN[:, m, k * Q:(k + 1) * Q],
                                                    start=(m == 0), stop=(m == TPB - 1))
                        last.then_inc(w_filled.sem, 1)
                if here(slot, 0):
                    pe.wait_ge(ln2_ready.sem, ln2_ready.after("ln2", slot))
                    transposed("ln2T", slot, lambda c: work_a[:, c, :])
                if here(slot, -1):
                    pe.wait_ge(ln3_ready.sem, ln3_ready.after("ln3", slot))
                    transposed("ln3T", slot, lambda c: work_b[:, c * P:(c + 1) * P])

            for s in range(first, TPB):
                stages(Slot(s))
            with pe.Fori(0, (batches - 2) // 2) as r:
                for s in range(TPB, 3 * TPB):
                    stages(Slot(s, r))
            for s in range(tiles - TPB, tiles + 2):
                stages(Slot(s))


def pass_b(nc, ctx, x3, w, ag, gate_b, b_up, bias, out):
    tiles = x3.shape[0] // P
    per_round = 4
    first = -2

    def sb(name, shape, dt=F32):
        return ctx.enter_context(nc.sbuf_tensor(name, shape, dt))

    def sem(name):
        return ctx.enter_context(nc.semaphore(name))

    wt = sb("wt", [P, DC + 1, 2 * D], F16)
    xt = sb("xt_b", [P, 4, D])
    ln = sb("ln", [P, D])
    lnT = sb("lnT", [P, 2, 2, DC, P], F16)
    ag_sb = sb("ag_sb", [P, 2, DC, AG], F16)
    up_sb = sb("up_sb", [MAXR + 1, D])
    ident = sb("ident_b", [P, P])
    order4 = sb("order4", [P, NG])
    least = sb("least", [P, MAXR])
    gb_sb = sb("gb_sb", [P, NG])
    consts = sb("consts_b", [P, 4])
    blockmax = sb("blockmax", [P, DC])
    tmax = sb("tmax", [P, 2])
    gmax = sb("gmax", [P, 2])
    pow2 = sb("pow2", [P, 2])
    pow2c = sb("pow2c", [P, 2])
    rpow2 = sb("rpow2", [P, 2])
    scale = sb("scale", [P, 2])
    unscale = sb("unscale", [P, 2])
    hm_scale = sb("hm_scale", [P, 1])
    st6 = sb("st6_b", [P, NQ, 6])
    mv = sb("mv_b", [P, 2])
    veps = sb("veps_b", [P, 1])
    rstd1 = sb("rstd1", [P, 1])
    rstd = sb("rstd_b", [P, 1])
    shift1 = sb("shift1_b", [P, 1])
    shift = sb("shift_b", [P, 1])
    fence = sb("fence_b", [P, 1])
    hs = sb("hs_b", [P, AG])
    gate = sb("gate", [P, 3, NG])
    small = sb("small", [P, 8])
    mask = sb("mask", [P, MAXR])
    hm = sb("hm", [P, MAXR + 1])
    hmT = sb("hmT", [MAXR + 1, P])
    tb = [ctx.enter_context(nc.psum_tensor(f"tbb{k}", [P, Q], F32)) for k in range(RING)]
    wb = [ctx.enter_context(nc.psum_tensor(f"wbb{k}", [P, Q], F32)) for k in range(RING)]

    def counted(name, stages):
        return Counted(sem(name), stages, tiles, per_round, first)

    T_STAGES = [("hmT", 1, 0), ("lnT", 4, 1)]
    W_STAGES = [("down", 1, 0), ("main", 4, 0)]
    t_filled = counted("bt_filled", T_STAGES)
    t_drained = counted("bt_drained", T_STAGES)
    w_filled = counted("bw_filled", W_STAGES)
    w_drained = counted("bw_drained", W_STAGES)
    high_ready = counted("high_ready", [("lnT", 4, 1)])
    steps = counted("bsteps", [("gate", 12, 0), ("ln", NQ, 1)])
    stats_ready = counted("bstats_ready", [("ln", 1, 1)])
    pool_steps = counted("bpool_steps", [("ln", 3, 1)])
    rstd_ready = counted("brstd_ready", [("ln", 1, 1)])
    ln_ready = counted("ln_ready", [("ln", 1, 1)])
    gexp_ready = counted("gexp_ready", [("gate", 1, 0)])
    x_loaded = [sem(f"bx_loaded{j}") for j in range(4)]
    x_stored = [sem(f"bx_stored{j}") for j in range(4)]
    w_loaded = [sem(f"w_loaded{j}") for j in range(4)]
    ag_loaded = sem("ag_loaded")
    const_loaded = sem("bconst_loaded")
    const_ready = sem("bconst_ready")
    ident_blank = sem("bident_blank")
    tmax_ready = sem("tmax_ready")
    gmax_ready = sem("gmax_ready")
    scale_steps = sem("scale_steps")
    high_split = sem("high_split")
    low_split = sem("low_split")

    def here(slot, offset):
        return 0 <= slot.n + offset < tiles

    def tile(slot, offset):
        return slot.n + offset + per_round * slot.rounds

    def schedule(eng, stages):
        for s in range(first, 4):
            stages(Slot(s))
        with eng.Fori(0, tiles // 4 - 2) as r:
            for s in range(4, 8):
                stages(Slot(s, r))
        for s in range(tiles - 4, tiles):
            stages(Slot(s))

    with nc.Block() as block:

        @block.sync
        def _(sp):
            sp.dma_start(ln[:, 0:DC * AG], ag.rearrange("p c a -> p (c a)")).then_inc(ag_loaded, 16)
            for c in range(DC):
                if c >= 4:
                    sp.wait_ge(w_loaded[c % 4], 16 * (c // 4))
                sp.dma_start(wt[:, c + 1, :].bitcast(F32), w[c * P:(c + 1) * P, :]).then_inc(w_loaded[c % 4], 16)
            sp.dma_start(up_sb[0:MAXR, :], b_up).then_inc(const_loaded, 16)
            sp.dma_start(up_sb[MAXR:MAXR + 1, :], bias).then_inc(const_loaded, 16)
            sp.dma_start(gb_sb[:], gate_b).then_inc(const_loaded, 16)

            def stages(slot):
                if here(slot, 2):
                    j = (slot.n + 2) % 4
                    if here(slot, -2):
                        sp.wait_ge(x_stored[j], 16 * ((slot.n + 2) // 4 + slot.rounds))
                    sp.dma_start(xt[:, j, :], x3[bass.ds(tile(slot, 2) * P, P), :]).then_inc(x_loaded[j], 16)
                if here(slot, 0):
                    wait(sp, w_drained.sem, w_drained.after("main", slot))
                    sp.dma_start(out[bass.ds(tile(slot, 0) * P, P), :], xt[:, slot.n % 4, :]
                                 ).then_inc(x_stored[slot.n % 4], 16)

            schedule(sp, stages)
            for j in range(4):
                sp.wait_ge(x_stored[j], 16 * (tiles // 4))

        @block.gpsimd
        def _(pool):
            nc.gpsimd.memset(ident[:], 0.0).then_inc(ident_blank, 1)
            for n, value in enumerate((EPS, -0.5, -1.0, XS)):
                nc.gpsimd.memset(consts[:, n:n + 1], value)
            for g in range(NG):
                nc.gpsimd.memset(order4[:, g:g + 1], float(NG - g))
                low = 0 if g == 0 else RANKS[g - 1]
                nc.gpsimd.memset(least[:, low:RANKS[g]], float(NG - g))
            pool.wait_ge(ident_blank, 1)
            nc.gpsimd.affine_select(out=ident[:], in_=ident[:], compare_op=ALU.not_equal, fill=1.0, base=0,
                                    pattern=[[-1, P]], channel_multiplier=1).then_inc(const_ready, 1)
            pool.wait_ge(tmax_ready, 2)
            nc.gpsimd.partition_all_reduce(gmax[:], tmax[:], P, bass.bass_isa.ReduceOp.absmax).then_inc(gmax_ready, 1)

            def stages(slot):
                if here(slot, 1):
                    base = pool_steps.before("ln", slot)
                    pool.wait_ge(stats_ready.sem, stats_ready.after("ln", slot))
                    nc.gpsimd.tensor_tensor(shift1[:], mv[:, 0:1], consts[:, 2:3], ALU.mult)
                    nc.gpsimd.tensor_tensor(veps[:], mv[:, 1:2], consts[:, 0:1], ALU.add).then_inc(pool_steps.sem, 1)
                    pool.wait_ge(pool_steps.sem, base + 1)
                    nc.gpsimd.tensor_tensor(rstd1[:], veps[:], consts[:, 1:2], ALU.pow).then_inc(pool_steps.sem, 1)
                    pool.wait_ge(pool_steps.sem, base + 2)
                    nc.gpsimd.tensor_tensor(rstd[:], rstd1[:], consts[:, 3:4], ALU.mult).then_inc(pool_steps.sem, 1)
                    pool.wait_ge(pool_steps.sem, base + 3)
                    nc.gpsimd.tensor_tensor(shift[:], shift1[:], rstd[:], ALU.mult).then_inc(rstd_ready.sem, 1)

            schedule(pool, stages)

        @block.scalar
        def _(act):
            act.wait_ge(scale_steps, 5)
            nc.scalar.activation(ag_sb[:, 0].rearrange("p c a -> p (c a)"), ln[:, 0:DC * AG], ACT.Copy,
                                 scale=scale[:, 1:2]).then_inc(high_split, 1)
            for c in range(DC):
                if c >= 1:
                    act.wait_ge(low_split, c + 1)
                nc.scalar.activation(wt[:, c, 0:D], wt[:, c + 1, :].bitcast(F32), ACT.Copy, scale=scale[:, 0:1]
                                     ).then_inc(high_split, 1)

            def stages(slot):
                if here(slot, 0):
                    act.wait_ge(steps.sem, steps.after("gate", slot, 2))
                    nc.scalar.activation(gate[:, 1, :], gate[:, 0, :], ACT.Exp, bias=small[:, 0:1],
                                         accum_out=small[:, 1:2]).then_inc(gexp_ready.sem, 1)
                if here(slot, 1):
                    if slot.n == -1:
                        act.wait_ge(low_split, 1)
                    else:
                        act.wait_ge(t_filled.sem, t_filled.after("lnT", slot.back(1)))
                    act.wait_ge(rstd_ready.sem, rstd_ready.after("ln", slot))
                    nc.scalar.activation(ln[:], xt[:, (slot.n + 1) % 4, :], ACT.Identity, scale=rstd[:], bias=shift[:]
                                         ).then_inc(ln_ready.sem, 1)
                    for k in range(4):
                        act.wait_ge(t_filled.sem, t_filled.after("lnT", slot, k + 1))
                        b = tb[t_filled.after("lnT", Slot(slot.n), k) % RING]
                        nc.scalar.activation(
                            lnT[:, (slot.n + 1) % 2, 0, 4 * k:4 * k + 4, :].rearrange("p a b -> p (a b)"), b[:], ACT.Copy
                        ).then_inc(high_ready.sem, 1)

            schedule(act, stages)

        @block.vector
        def _(dve):
            dve.wait_ge(ag_loaded, 16)
            nc.vector.tensor_reduce(tmax[:, 1:2], ln[:, 0:DC * AG], AX_X, ALU.max, apply_absolute_value=True
                                    ).then_inc(tmax_ready, 1)
            for c in range(DC):
                dve.wait_ge(w_loaded[c % 4], 16 * (c // 4 + 1))
                last = nc.vector.tensor_reduce(blockmax[:, c:c + 1], wt[:, c + 1, :].bitcast(F32), AX_X, ALU.max,
                                               apply_absolute_value=True)
            last.then_inc(scale_steps, 1)
            dve.wait_ge(scale_steps, 1)
            nc.vector.tensor_reduce(tmax[:, 0:1], blockmax[:], AX_X, ALU.max).then_inc(tmax_ready, 1)
            dve.wait_ge(gmax_ready, 1)
            nc.vector.tensor_scalar(pow2[:].bitcast(U32), gmax[:].bitcast(U32), 0x7F800000, None, ALU.bitwise_and
                                    ).then_inc(scale_steps, 1)
            dve.wait_ge(scale_steps, 2)
            nc.vector.tensor_scalar(pow2c[:], pow2[:], 2.0 ** -100, None, ALU.max).then_inc(scale_steps, 1)
            dve.wait_ge(scale_steps, 3)
            nc.vector.reciprocal(rpow2[:], pow2c[:]).then_inc(scale_steps, 1)
            nc.vector.tensor_scalar(unscale[:], pow2c[:], 1.0 / (TOP * XS), None, ALU.mult)
            dve.wait_ge(scale_steps, 4)
            nc.vector.tensor_scalar(scale[:], rpow2[:], TOP, None, ALU.mult).then_inc(scale_steps, 1)
            dve.wait_ge(scale_steps, 5)
            nc.vector.tensor_scalar(hm_scale[:], scale[:, 0:1], XS, None, ALU.mult).then_inc(scale_steps, 1)
            nc.vector.tensor_scalar(hm[:, MAXR:MAXR + 1], scale[:, 0:1], XS, None, ALU.mult).then_inc(scale_steps, 1)
            dve.wait_ge(scale_steps, 7)
            dve.wait_ge(high_split, 1)
            nc.vector.scalar_tensor_tensor(ag_sb[:, 1].rearrange("p c a -> p (c a)"), ln[:, 0:DC * AG], scale[:, 1:2],
                                           ag_sb[:, 0].rearrange("p c a -> p (c a)"), ALU.mult, ALU.subtract
                                           ).then_inc(low_split, 1)
            for c in range(DC):
                dve.wait_ge(high_split, c + 2)
                nc.vector.scalar_tensor_tensor(wt[:, c, D:2 * D], wt[:, c + 1, :].bitcast(F32), scale[:, 0:1],
                                               wt[:, c, 0:D], ALU.mult, ALU.subtract).then_inc(low_split, 1)
            dve.wait_ge(const_ready, 1)
            dve.wait_ge(const_loaded, 48)

            def bank(stage, slot, k):
                return wb[w_filled.after(stage, Slot(slot.n), k) % RING]

            def main(slot, k):
                part = xt[:, slot.n % 4, k * Q:(k + 1) * Q]
                dve.wait_ge(w_filled.sem, w_filled.after("main", slot, k + 1))
                nc.vector.scalar_tensor_tensor(part, bank("main", slot, k)[:], unscale[:, 0:1], part, ALU.mult, ALU.add
                                               ).then_inc(w_drained.sem, 1)

            def stages(slot):
                if here(slot, 0):
                    base = steps.before("gate", slot)
                    done = 0

                    def step(ins):
                        nonlocal done
                        done += 1
                        ins.then_inc(steps.sem, 1)
                        dve.wait_ge(steps.sem, base + done)

                    dve.wait_ge(w_filled.sem, w_filled.after("down", slot))
                    nc.vector.tensor_scalar(hs[:], bank("down", slot, 0)[:, 0:AG], unscale[:, 1:2], None, ALU.mult
                                            ).then_inc(w_drained.sem, 1)
                    dve.wait_ge(w_drained.sem, w_drained.after("down", slot))
                    step(nc.vector.tensor_tensor(gate[:, 0, :], hs[:, MAXR:], gb_sb[:], ALU.add))
                    step(nc.vector.tensor_reduce(small[:, 0:1], gate[:, 0, :], AX_X, ALU.max, negate=True))
                    dve.wait_ge(gexp_ready.sem, gexp_ready.after("gate", slot))
                    step(nc.vector.reciprocal(small[:, 2:3], small[:, 1:2]))
                    step(nc.vector.tensor_scalar(gate[:, 0, :], gate[:, 1, :], small[:, 2:3], None, ALU.mult))
                    step(nc.vector.tensor_reduce(small[:, 3:4], gate[:, 0, :], AX_X, ALU.max))
                    step(nc.vector.scalar_tensor_tensor(gate[:, 2, :], gate[:, 0, :], small[:, 3:4], order4[:],
                                                        ALU.is_equal, ALU.mult))
                    step(nc.vector.reciprocal(small[:, 4:5], small[:, 3:4]))
                    step(nc.vector.tensor_tensor(small[:, 5:6], small[:, 3:4], small[:, 4:5], ALU.mult))
                    step(nc.vector.tensor_reduce(small[:, 6:7], gate[:, 2, :], AX_X, ALU.max))
                    step(nc.vector.tensor_scalar(mask[:], least[:], small[:, 6:7], small[:, 5:6], ALU.is_ge, ALU.mult))
                    step(nc.vector.tensor_scalar(hs[:, 0:MAXR], hs[:, 0:MAXR], hm_scale[:], None, ALU.mult))
                    step(nc.vector.tensor_tensor(hm[:, 0:MAXR], hs[:, 0:MAXR], mask[:], ALU.mult))
                if here(slot, 1):
                    j1 = (slot.n + 1) % 4
                    base = steps.before("ln", slot)
                    dve.wait_ge(x_loaded[j1], 16 * ((slot.n + 1) // 4 + slot.rounds) + 16)
                    for k in range(NQ):
                        nc.vector.bn_stats(st6[:, k, :], xt[:, j1, k * Q:(k + 1) * Q]).then_inc(steps.sem, 1)
                    dve.wait_ge(steps.sem, base + NQ)
                    nc.vector.memset(fence[:], 0.0)
                    nc.vector.bn_aggr(mv[:], st6[:]).then_inc(stats_ready.sem, 1)
                if here(slot, 0):
                    dve.wait_ge(t_filled.sem, t_filled.after("hmT", slot))
                    b = tb[t_filled.before("hmT", Slot(slot.n)) % RING]
                    nc.vector.tensor_copy(hmT[:], b[0:MAXR + 1, 0:P]).then_inc(t_drained.sem, 1)
                    for k in range(3):
                        main(slot, k)
                if here(slot, 1):
                    for k in range(4):
                        dve.wait_ge(high_ready.sem, high_ready.after("lnT", slot, k + 1))
                        b = tb[t_filled.after("lnT", Slot(slot.n), k) % RING]
                        two = [lnT[:, (slot.n + 1) % 2, h, 4 * k:4 * k + 4, :].rearrange("p a b -> p (a b)")
                               for h in range(2)]
                        nc.vector.tensor_tensor(two[1], b[:], two[0], ALU.subtract).then_inc(t_drained.sem, 1)
                if here(slot, 0):
                    main(slot, 3)

            schedule(dve, stages)

        @block.tensor
        def _(pe):
            pe.wait_ge(const_ready, 1)

            def t_bank(stage, slot, k):
                wait(pe, t_drained.sem, t_filled.after(stage, slot, k) - RING + 1)
                return tb[t_filled.after(stage, Slot(slot.n), k) % RING]

            def w_bank(stage, slot, k):
                wait(pe, w_drained.sem, w_filled.after(stage, slot, k) - RING + 1)
                return wb[w_filled.after(stage, Slot(slot.n), k) % RING]

            def split_product(dst, slot, rhs, stop):
                for c in range(DC):
                    for n, (hl, hr) in enumerate(((0, 0), (0, 1), (1, 0))):
                        last = nc.tensor.matmul(dst, lnT[:, slot.n % 2, hl, c, :], rhs(hr, c),
                                                start=(c == 0 and n == 0), stop=(stop and c == DC - 1 and n == 2))
                return last

            def main(slot, k):
                b = w_bank("main", slot, k)
                split_product(b[:], slot, lambda h, c: wt[:, c, h * D + k * Q:h * D + (k + 1) * Q], False)
                return b

            def lora_up(b, k):
                nc.tensor.matmul(b[:], hmT[:], up_sb[:, k * Q:(k + 1) * Q], start=False, stop=True
                                 ).then_inc(w_filled.sem, 1)

            def stages(slot):
                if here(slot, 0):
                    pe.wait_ge(t_drained.sem, t_drained.after("lnT", slot.back(1)))
                    b = w_bank("down", slot, 0)
                    split_product(b[:, 0:AG], slot, lambda h, c: ag_sb[:, h, c, :], True).then_inc(w_filled.sem, 1)
                    if slot.n == 0:
                        pe.wait_ge(low_split, DC + 1)
                        pe.wait_ge(const_loaded, 48)
                    b0 = main(slot, 0)
                    pe.wait_ge(steps.sem, steps.after("gate", slot))
                    t = t_bank("hmT", slot, 0)
                    nc.tensor.transpose(t[0:MAXR + 1, 0:P], hm[:], ident[:]).then_inc(t_filled.sem, 1)
                    b1 = main(slot, 1)
                    pe.wait_ge(t_drained.sem, t_drained.after("hmT", slot))
                    lora_up(b0, 0)
                    lora_up(b1, 1)
                    lora_up(main(slot, 2), 2)
                if here(slot, 1):
                    pe.wait_ge(ln_ready.sem, ln_ready.after("ln", slot))
                    for k in range(4):
                        b = t_bank("lnT", slot, k)
                        for m in range(4):
                            c = 4 * k + m
                            last = nc.tensor.transpose(b[:, m * P:(m + 1) * P], ln[:, c * P:(c + 1) * P], ident[:])
                        last.then_inc(t_filled.sem, 1)
                if here(slot, 0):
                    lora_up(main(slot, 3), 3)

            schedule(pe, stages)


def program(nc, x, c_rows, c_cols, ra, bwt, w, ag, gate_b, b_up, bias, out):
    x3 = nc.dram_tensor("x3", x.shape, F32, kind="Internal").ap()
    with ExitStack() as ctx:
        pass_a(nc, ctx, x, c_rows, c_cols, ra, bwt, x3)
    with ExitStack() as ctx:
        pass_b(nc, ctx, x3, w, ag, gate_b, b_up, bias, out)


def kernel(x, ctx_4096, L0_ffn_route_w, L0_ffn_A, L0_ffn_Bw, L1_ffn_W, L1_ffn_b, L1_ffn_A, L1_ffn_B,
           L1_ffn_gate_w, L1_ffn_gate_b):
    import numpy as np
    from concourse import bacc
    from concourse.bass_utils import run_bass_kernel_spmd

    shape = x.shape
    batches = shape[0]
    rows = batches * ROWS
    c = np.asarray(ctx_4096)

    def blocks(a):
        return np.ascontiguousarray(a.T.reshape(DC, P, a.shape[0]).transpose(1, 0, 2))

    arrays = {
        "x": np.ascontiguousarray(np.asarray(x).reshape(rows, D)),
        "c_rows": np.ascontiguousarray(c.reshape(rows, D)),
        "c_cols": np.ascontiguousarray(c.reshape(batches, ROWS, DC, P).transpose(0, 3, 2, 1).reshape(batches * P, DC, ROWS)),
        "ra": blocks(np.concatenate([np.asarray(L0_ffn_route_w), np.asarray(L0_ffn_A).reshape(ER, D)])),
        "bwt": np.ascontiguousarray(np.asarray(L0_ffn_Bw).transpose(0, 2, 1).reshape(ER, D)),
        "w": np.ascontiguousarray(np.asarray(L1_ffn_W).T),
        "ag": blocks(np.concatenate([np.asarray(L1_ffn_A), np.asarray(L1_ffn_gate_w)])),
        "gate_b": np.ascontiguousarray(np.broadcast_to(np.asarray(L1_ffn_gate_b), (P, NG))),
        "b_up": np.ascontiguousarray(np.asarray(L1_ffn_B).T),
        "bias": np.ascontiguousarray(np.asarray(L1_ffn_b).reshape(1, D)),
    }
    nc = bacc.Bacc("TRN2", target_bir_lowering=False, num_devices=1)
    aps = {n: nc.dram_tensor(n, a.shape, F32, kind="ExternalInput").ap() for n, a in arrays.items()}
    out = nc.dram_tensor("out", (rows, D), F32, kind="ExternalOutput").ap()
    program(nc, **aps, out=out)
    result = run_bass_kernel_spmd(nc, [arrays], core_ids=[0])
    return result.results[0]["out"].reshape(shape)
```

```python
from contextlib import ExitStack

import concourse.bass as bass
from concourse import mybir

F32 = mybir.dt.float32
F16 = mybir.dt.float16
BF16 = mybir.dt.bfloat16
U32 = mybir.dt.uint32
ALU = mybir.AluOpType
ACT = mybir.ActivationFunctionType
AX_X = mybir.AxisListType.X

P = 128
D = 2048
DC = D // P
ROWS = 512
TPB = ROWS // P
HD = 64
Q = 512
NQ = D // Q
E = 8
R = 16
ER = E * R
EPS = 1e-5
RING = 4
NUM = 2 * HD + 2
NUM_FILLS = [3, 3, 3, 3, 3, 1]
MAXR = 64
NG = 4
RANKS = (8, 16, 32, 64)
AG = MAXR + NG
CTOP = 2.0 ** 14
PS = 4096.0
XS = 64.0
TOP = 4096.0


class Slot:

    def __init__(self, n, rounds=0):
        self.n, self.rounds = n, rounds

    def back(self, k):
        return Slot(self.n - k, self.rounds)


class Counted:

    def __init__(self, sem, stages, tiles, slots_per_round, first):
        self.sem, self.stages, self.tiles, self.first = sem, stages, tiles, first
        self.per_round = slots_per_round * sum(k for _, k, _ in stages)

    def _count(self, slot, stage, k):
        total = 0
        for s in range(self.first, slot.n + 1):
            for name, raises, offset in self.stages:
                if s == slot.n and name == stage:
                    total += k
                    return total + slot.rounds * self.per_round
                if 0 <= s + offset < self.tiles:
                    total += raises
        raise KeyError(stage)

    def before(self, stage, slot):
        return self._count(slot, stage, 0)

    def after(self, stage, slot, k=None):
        if k is None:
            k = next(r for name, r, _ in self.stages if name == stage)
        return self._count(slot, stage, k)


class Banks:

    def __init__(self, nc, ctx, name, filled):
        self.filled = filled
        self.banks = [ctx.enter_context(nc.psum_tensor(f"{name}_bank{k}", [P, Q], F32)) for k in range(RING)]
        self.emptied = [ctx.enter_context(nc.semaphore(f"{name}_emptied{k}")) for k in range(RING)]

    def _fill(self, stage, slot, k):
        return self.filled.before(stage, Slot(slot.n)) + k

    def bank(self, stage, slot, k=0):
        return self.banks[self._fill(stage, slot, k) % RING]

    def sem(self, stage, slot, k=0):
        return self.emptied[self._fill(stage, slot, k) % RING]

    def wait_filled(self, eng, stage, slot, k=0):
        eng.wait_ge(self.filled.sem, self.filled.after(stage, slot, k + 1))

    def wait_read(self, eng, stage, slot, k=0):
        fill = self._fill(stage, slot, k)
        eng.wait_ge(self.emptied[fill % RING], fill // RING + 1 + slot.rounds * (self.filled.per_round // RING))

    def take(self, eng, stage, slot, k=0):
        fill = self._fill(stage, slot, k)
        if fill >= RING:
            eng.wait_ge(self.emptied[fill % RING], fill // RING + slot.rounds * (self.filled.per_round // RING))
        return self.banks[fill % RING]


class InPlace:

    def __init__(self, units):
        self.units = units

    @staticmethod
    def shape(blocks):
        return [2 * blocks + 2, Q]

    def raw(self, c, n=1):
        return self.units[:, 2 * c + 2:2 * (c + n) + 2, :].rearrange("p (c h) m -> p c (h m)", h=2).bitcast(F32)

    def half(self, h, c):
        return self.units[:, 2 * c + 2 if h else max(2 * c - 1, 0), :]


def split_high(nc, act, buf, c, scale, high_done, low_done, done):
    if c >= 2:
        act.wait_ge(low_done, done + c - 1)
    elif c == 0:
        wait(act, low_done, done)
    nc.scalar.activation(buf.half(0, c), buf.raw(c)[:, 0, :], ACT.Copy, scale=scale).then_inc(high_done, 1)


def split_low(nc, dve, buf, c, scale, high_done, low_done, done):
    dve.wait_ge(high_done, done + c + 1)
    nc.vector.scalar_tensor_tensor(buf.half(1, c), buf.raw(c)[:, 0, :], scale, buf.half(0, c),
                                   ALU.mult, ALU.subtract).then_inc(low_done, 1)


def split_product(nc, dst, left, right, blocks, stop=True):
    for c in range(blocks):
        for n, (hl, hr) in enumerate(((0, 0), (0, 1), (1, 0))):
            last = nc.tensor.matmul(dst, left(hl, c), right(hr, c), start=(c == 0 and n == 0),
                                    stop=(stop and c == blocks - 1 and n == 2))
    return last


def wait(eng, sem, value):
    if isinstance(value, int) and value <= 0:
        return
    eng.wait_ge(sem, value)


def pass_a(nc, ctx, x, c_rows, c_cols, ra, bwt, w, ag, wmax, x3):
    batches = x.shape[0] // ROWS
    tiles = batches * TPB
    share = DC * D // tiles
    cuts = D // share
    per_round = 2 * TPB
    first = -2

    def sb(name, shape, dt=F32):
        return ctx.enter_context(nc.sbuf_tensor(name, shape, dt))

    def sem(name):
        return ctx.enter_context(nc.semaphore(name))

    ctxT_units = sb("ctxT", [P, 2] + InPlace.shape(DC), F16)
    ctxT = [InPlace(ctxT_units[:, p]) for p in range(2)]
    ctxN = InPlace(sb("ctxN", [P] + InPlace.shape(NQ * TPB), F16))
    xt = sb("xt", [P, TPB, D])
    crow = sb("crow", [P, D])
    expT = sb("expT", [P, 2, DC, P], F16)
    work_a = sb("work_a", [P, DC, P])
    work_b = sb("work_b", [P, D])
    ln2T = sb("ln2T", [P, DC, P])
    ln3T = sb("ln3T", [P, 2, DC, P], F16)
    ra_sb = sb("ra_sb", [P, DC, E + ER])
    bwt_sb = sb("bwt_sb", [ER, D])
    kv = sb("kv", [P, 2, NUM])
    prob = sb("prob", [P, ROWS])
    probT = sb("probT", [P, 2, TPB, P], F16)
    wh = sb("wh", [P, ER])
    whT = sb("whT", [ER, P])
    hs = sb("hs", [P, E + ER])
    ident = sb("ident", [P, P])
    order8 = sb("order8", [P, E])
    consts = sb("consts", [P, 4])
    csums = sb("csums", [P, DC])
    cbound = sb("cbound", [P, 1])
    gbound = sb("gbound", [P, 1])
    pool_fence = sb("pool_fence", [P, 1])
    cpow2 = sb("cpow2", [P, 1])
    cpow2c = sb("cpow2c", [P, 1])
    crpow2 = sb("crpow2", [P, 1])
    cscale = sb("cscale", [P, 2])
    unscore = sb("unscore", [P, 2])
    unexp = sb("unexp", [P, 2])
    st6 = sb("st6", [P, 3, NQ, 6])
    mv = sb("mv", [P, 3, 2])
    veps = sb("veps", [P, 3])
    rstd = sb("rstd", [P, 3])
    rstd3 = sb("rstd3", [P, 1])
    shift1 = sb("shift1", [P, 3])
    shift = sb("shift", [P, 3])
    fence = sb("fence", [P, 1])
    rden = sb("rden", [P, DC, 2])
    route = sb("route", [P, 4, E])
    ncmax = sb("ncmax", [P, 1])
    csum = sb("csum", [P, 2])
    rcsum = sb("rcsum", [P, 1])
    nsmax = sb("nsmax", [P, 1])
    sbias = sb("sbias", [P, 1])
    rkv = sb("rkv", [P, 1])
    rpv = sb("rpv", [P, 1])
    psum_row = sb("psum_row", [P, 1])
    rprob = sb("rprob", [P, 1])
    def counted(name, stages):
        return Counted(sem(name), stages, tiles, per_round, first)

    T_STAGES = [("expT", 4, 1), ("scores", 1, -2), ("whT", 1, -1), ("probT", 1, -2), ("ln2T", 4, 0), ("ln3T", 4, -1)]
    W_STAGES = [("down", 1, -1), ("num", 6, 0), ("attn1", 4, 0), ("kvs", 1, 1), ("up", 4, -1), ("pv", 4, -2)]
    tbank = Banks(nc, ctx, "t", counted("t_filled", T_STAGES))
    wbank = Banks(nc, ctx, "w", counted("w_filled", W_STAGES))
    steps = counted("steps", [("down", 4, -1), ("num", 6, 0), ("scores", 1, -2), ("attn1", 4, 0),
                              ("kvs", 2, 1), ("up", 4, -1), ("ln1", 4, 1), ("pv", 2, -2)])
    stats_ready = counted("stats_ready", [("attn1", 1, 0), ("up", 1, -1), ("ln1", 1, 1)])
    pool_steps = counted("pool_steps", [("attn1", 2, 0), ("up", 3, -1), ("ln1", 2, 1)])
    high_ready = counted("t_high", [("expT", 4, 1), ("probT", 1, -2), ("ln3T", 4, -1)])
    scan_loaded = counted("scan_loaded", [("scan", 16, 0)])
    scanned = counted("scanned", [("scan", 1, 0)])
    rstd_ready = counted("rstd_ready", [("attn1", 1, 0), ("up", 1, -1), ("ln1", 1, 1)])
    wh_ready = counted("wh_ready", [("down", 1, -1)])
    smax_ready = counted("smax_ready", [("scores", 1, -2)])
    cmax_ready = counted("cmax_ready", [("cexp", 1, 2)])
    cexp_ready = counted("cexp_ready", [("cexp", 1, 2)])
    q_ready = counted("q_ready", [("q", 1, 1)])
    ln2_ready = counted("ln2_ready", [("ln2", 1, 0)])
    ln3_ready = counted("ln3_ready", [("ln3", 1, -1)])
    c_loaded = counted("c_loaded", [("load", 16, 2)])
    x_loaded = [sem(f"x_loaded{j}") for j in range(TPB)]
    x_stored = [sem(f"x_stored{j}") for j in range(TPB)]
    t_loaded = [sem(f"t_loaded{j}") for j in range(NQ)]
    n_loaded = [sem(f"n_loaded{j}") for j in range(NQ)]
    const_loaded = sem("const_loaded")
    const_ready = sem("const_ready")
    ident_blank = sem("ident_blank")
    csums_ready = sem("csums_ready")
    t_high = sem("ctxT_high")
    t_low = sem("ctxT_low")
    n_high = sem("ctxN_high")
    n_low = sem("ctxN_low")
    cbound_ready = sem("cbound_ready")
    gbound_ready = sem("gbound_ready")
    cscale_steps = sem("cscale_steps")
    cscale_ready = sem("cscale_ready")
    ag_loaded = sem("ag_loaded")
    ag_scanned = sem("ag_scanned")
    kv_blank = sem("kv_blank")

    LN1, LN2, LN3 = 0, 1, 2
    B_EARLY, T_EARLY, N_EARLY = 8, 4, 12

    def batch(slot, offset):
        return (slot.n + offset) // TPB + 2 * slot.rounds, (slot.n + offset) % TPB

    def here(slot, offset):
        return 0 <= slot.n + offset < tiles

    with nc.Block() as block:

        @block.sync
        def _(sp):
            def load_cols(b, parity):
                for k in range(NQ):
                    sp.dma_start(ctxT[parity].raw(4 * k, 4), c_cols[bass.ds(b * P, P), k * 4:k * 4 + 4, :]
                                 ).then_inc(t_loaded[k], 16)

            def load_x(b, j):
                sp.dma_start(xt[:, j, :], x[bass.ds(b * ROWS + j * P, P), :]).then_inc(x_loaded[j], 16)

            def stages(slot):
                if here(slot, 2):
                    b, j = batch(slot, 2)
                    if here(slot, 1):
                        tbank.wait_read(sp, "expT", slot, 3)
                    sp.dma_start(crow[:], c_rows[bass.ds(b * ROWS + j * P, P), :]).then_inc(c_loaded.sem, 16)
                if slot.n == first:
                    load_x(0, 0)
                    load_cols(0, 0)
                    sp.dma_start(ra_sb[:], ra).then_inc(const_loaded, 16)
                    sp.dma_start(bwt_sb[:], bwt).then_inc(const_loaded, 16)
                    sp.dma_start(ln2T[:].rearrange("p c a -> p (c a)")[:, 0:DC * AG], ag.rearrange("p c a -> p (c a)")
                                 ).then_inc(ag_loaded, 16)
                    for k in range(NQ):
                        sp.dma_start(ctxN.raw(4 * k, 4),
                                     c_rows[0:ROWS, k * Q:(k + 1) * Q].rearrange("(a p) n -> p a n", p=P)
                                     ).then_inc(n_loaded[k], 16)
                if slot.n == 0:
                    load_cols(1, 1)
                b, j = batch(slot, 0)
                if here(slot, 0):
                    if here(slot, -1):
                        wbank.wait_filled(sp, "down", slot)
                    else:
                        sp.wait_ge(ag_scanned, 1)
                    sp.dma_start(ln2T[:].rearrange("p c a -> p (c a)")[:, 0:share],
                                 w[bass.ds((slot.n // cuts + slot.rounds * (per_round // cuts)) * P, P),
                                   slot.n % cuts * share:(slot.n % cuts + 1) * share]).then_inc(scan_loaded.sem, 16)
                if slot.n >= TPB and j == 1 and here(slot, TPB):
                    tbank.wait_filled(sp, "scores", slot)
                    load_cols(b + 1, (slot.n // TPB + 1) % 2)
                if slot.n >= TPB and j == 1 and here(slot, 0):
                    for k in range(NQ):
                        wbank.wait_filled(sp, "pv", slot, min(k + 1, NQ - 1))
                        sp.dma_start(ctxN.raw(4 * k, 4),
                                     c_rows[bass.ds(b * ROWS, ROWS), k * Q:(k + 1) * Q].rearrange("(a p) n -> p a n", p=P)
                                     ).then_inc(n_loaded[k], 16)
                if here(slot, -2):
                    bs, js = batch(slot, -2)
                    wbank.wait_read(sp, "pv", slot, NQ - 1)
                    sp.dma_start(x3[bass.ds(bs * ROWS + js * P, P), :], xt[:, js, :]).then_inc(x_stored[js], 16)
                if slot.n > first and here(slot, 2):
                    bl, jl = batch(slot, 2)
                    if here(slot, -2):
                        sp.wait_ge(x_stored[jl], bl * 16)
                    load_x(bl, jl)

            for s in range(first, TPB):
                stages(Slot(s))
            with sp.Fori(0, (batches - 2) // 2) as r:
                for s in range(TPB, 3 * TPB):
                    stages(Slot(s, r))
            for s in range(tiles - TPB, tiles + 2):
                stages(Slot(s))
            for j in range(TPB):
                sp.wait_ge(x_stored[j], batches * 16)

        @block.gpsimd
        def _(pool):
            nc.gpsimd.memset(ident[:], 0.0).then_inc(ident_blank, 1)
            for n, value in enumerate((EPS, -0.5, -1.0, XS)):
                nc.gpsimd.memset(consts[:, n:n + 1], value)
            for e in range(E):
                nc.gpsimd.memset(order8[:, e:e + 1], float(E - e))
            pool.wait_ge(ident_blank, 1)
            nc.gpsimd.affine_select(out=ident[:], in_=ident[:], compare_op=ALU.not_equal, fill=1.0, base=0,
                                    pattern=[[-1, P]], channel_multiplier=1).then_inc(const_ready, 1)

            def layernorm_scale(slot, stage, which):
                base = pool_steps.before(stage, slot)
                one = slice(which, which + 1)
                pool.wait_ge(stats_ready.sem, stats_ready.after(stage, slot))
                nc.gpsimd.tensor_tensor(shift1[:, one], mv[:, which, 0:1], consts[:, 2:3], ALU.mult)
                nc.gpsimd.tensor_tensor(veps[:, one], mv[:, which, 1:2], consts[:, 0:1], ALU.add
                                        ).then_inc(pool_steps.sem, 1)
                pool.wait_ge(pool_steps.sem, base + 1)
                power = rstd3[:] if which == LN3 else rstd[:, one]
                nc.gpsimd.tensor_tensor(power, veps[:, one], consts[:, 1:2], ALU.pow).then_inc(pool_steps.sem, 1)
                pool.wait_ge(pool_steps.sem, base + 2)
                if which == LN3:
                    nc.gpsimd.tensor_tensor(rstd[:, one], power, consts[:, 3:4], ALU.mult).then_inc(pool_steps.sem, 1)
                    pool.wait_ge(pool_steps.sem, base + 3)
                nc.gpsimd.tensor_tensor(shift[:, one], shift1[:, one], rstd[:, one], ALU.mult
                                        ).then_inc(rstd_ready.sem, 1)

            def stages(slot):
                if here(slot, 0):
                    layernorm_scale(slot, "attn1", LN2)
                if here(slot, -1):
                    layernorm_scale(slot, "up", LN3)
                b, j = batch(slot, TPB)
                if j == 2 and here(slot, 2):
                    pool.wait_ge(cbound_ready, b + 1)
                    nc.gpsimd.tensor_tensor(pool_fence[:], consts[:, 0:1], consts[:, 1:2], ALU.mult)
                    nc.gpsimd.partition_all_reduce(gbound[:], cbound[:], P, bass.bass_isa.ReduceOp.absmax
                                                   ).then_inc(gbound_ready, 1)
                if here(slot, 1):
                    layernorm_scale(slot, "ln1", LN1)

            for s in range(first, TPB):
                stages(Slot(s))
            with pool.Fori(0, (batches - 2) // 2) as r:
                for s in range(TPB, 3 * TPB):
                    stages(Slot(s, r))
            for s in range(tiles - TPB, tiles + 2):
                stages(Slot(s))

        @block.scalar
        def _(act):
            def empty(stage, slot, dst):
                for k in range(4):
                    tbank.wait_filled(act, stage, slot, k)
                    nc.scalar.activation(dst[:, 4 * k:4 * k + 4, :].rearrange("p a b -> p (a b)"),
                                         tbank.bank(stage, slot, k)[:], ACT.Copy).then_inc(tbank.sem(stage, slot, k), 1)

            def high(stage, slot, dst, fills, scale=1.0):
                for k in range(fills):
                    tbank.wait_filled(act, stage, slot, k)
                    nc.scalar.activation(dst[:, 0, 4 * k:4 * k + 4, :].rearrange("p a b -> p (a b)"),
                                         tbank.bank(stage, slot, k)[:], ACT.Copy, scale=scale
                                         ).then_inc(high_ready.sem, 1)

            def bound_cols(b, p, blocks):
                for c in blocks:
                    if c % 4 == 0:
                        act.wait_ge(t_loaded[c // 4], b * 16 + 16)
                    if c > 1:
                        act.wait_ge(csums_ready, b * DC + c - 1)
                    nc.scalar.activation(ctxT[p].units[:, c % 2, :].bitcast(BF16), ctxT[p].raw(c)[:, 0, :], ACT.Abs,
                                         accum_out=csums[:, c:c + 1]).then_inc(csums_ready, 1)

            def split_cols(b, p, blocks):
                act.wait_ge(cscale_ready, b + 1)
                for c in blocks:
                    split_high(nc, act, ctxT[p], c, cscale[:, p:p + 1], t_high, t_low, b * DC)

            def split_rows(b, p, blocks):
                for c in blocks:
                    if c % TPB == 0:
                        act.wait_ge(n_loaded[c // TPB], b * 16 + 16)
                    split_high(nc, act, ctxN, c, cscale[:, p:p + 1], n_high, n_low, b * DC)

            def stages(slot):
                b, j = batch(slot, TPB)
                p = (slot.n // TPB + 1) % 2
                if here(slot, 1):
                    high("expT", slot, expT, 4, scale=PS)
                if j == 3 and here(slot, 1):
                    split_cols(b, p, range(T_EARLY, DC))
                if j == 2 and here(slot, -2):
                    split_rows(b - 1, 1 - p, range(N_EARLY))
                if here(slot, -2):
                    act.wait_ge(smax_ready.sem, smax_ready.after("scores", slot))
                    nc.scalar.activation(prob[:], tbank.bank("scores", slot)[:], ACT.Exp, bias=sbias[:],
                                         scale=unscore[:, (slot.n - 2) // TPB % 2:(slot.n - 2) // TPB % 2 + 1],
                                         accum_out=psum_row[:]).then_inc(tbank.sem("scores", slot), 1)
                if here(slot, -1):
                    tbank.wait_filled(act, "whT", slot)
                    nc.scalar.activation(whT[:], tbank.bank("whT", slot)[:, 0:P], ACT.Copy
                                         ).then_inc(tbank.sem("whT", slot), 1)
                if here(slot, -2):
                    high("probT", slot, probT, 1, scale=PS)
                if j == 2 and here(slot, -2):
                    split_rows(b - 1, 1 - p, range(N_EARLY, NQ * TPB))
                if here(slot, TPB) and slot.n > 0 and j == 1:
                    bound_cols(b, p, range(B_EARLY))
                if here(slot, 2) and j == 2 and slot.n > 0:
                    bound_cols(b, p, range(B_EARLY, DC))
                if here(slot, 2):
                    par = slot.n % 2
                    act.wait_ge(cmax_ready.sem, cmax_ready.after("cexp", slot))
                    nc.scalar.activation(crow[:], crow[:], ACT.Exp, bias=ncmax[:], accum_out=csum[:, par:par + 1]
                                         ).then_inc(cexp_ready.sem, 1)
                if slot.n == first:
                    bound_cols(0, 0, range(DC))
                if here(slot, 0):
                    act.wait_ge(rstd_ready.sem, rstd_ready.after("attn1", slot))
                    nc.scalar.activation(work_a[:].rearrange("p a b -> p (a b)"), xt[:, slot.n % TPB, :], ACT.Identity,
                                         scale=rstd[:, LN2:LN2 + 1], bias=shift[:, LN2:LN2 + 1]
                                         ).then_inc(ln2_ready.sem, 1)
                if here(slot, -1):
                    act.wait_ge(rstd_ready.sem, rstd_ready.after("up", slot))
                    nc.scalar.activation(work_b[:], xt[:, (slot.n - 1) % TPB, :], ACT.Identity,
                                         scale=rstd[:, LN3:LN3 + 1], bias=shift[:, LN3:LN3 + 1]
                                         ).then_inc(ln3_ready.sem, 1)
                if here(slot, 0):
                    act.wait_ge(scanned.sem, scanned.after("scan", slot))
                    empty("ln2T", slot, ln2T)
                if here(slot, -1):
                    high("ln3T", slot, ln3T, 4)
                if here(slot, 1):
                    act.wait_ge(rstd_ready.sem, rstd_ready.after("ln1", slot))
                    nc.scalar.activation(work_b[:], xt[:, (slot.n + 1) % TPB, :], ACT.Exp,
                                         scale=rstd[:, LN1:LN1 + 1], bias=shift[:, LN1:LN1 + 1]
                                         ).then_inc(q_ready.sem, 1)
                if j == 2 and here(slot, 2):
                    split_cols(b, p, range(T_EARLY))

            for s in range(first, TPB):
                stages(Slot(s))
            with act.Fori(0, (batches - 2) // 2) as r:
                for s in range(TPB, 3 * TPB):
                    stages(Slot(s, r))
            for s in range(tiles - TPB, tiles + 2):
                stages(Slot(s))

        @block.vector
        def _(dve):
            def low(stage, slot, dst, fills, scale=None):
                for k in range(fills):
                    dve.wait_ge(high_ready.sem, high_ready.after(stage, slot, k + 1))
                    halves = [dst[:, h, 4 * k:4 * k + 4, :].rearrange("p a b -> p (a b)") for h in range(2)]
                    b = tbank.bank(stage, slot, k)[:]
                    if scale is None:
                        ins = nc.vector.tensor_tensor(halves[1], b, halves[0], ALU.subtract)
                    else:
                        ins = nc.vector.scalar_tensor_tensor(halves[1], b, scale, halves[0], ALU.mult, ALU.subtract)
                    ins.then_inc(tbank.sem(stage, slot, k), 1)

            def add_and_stats(slot, stage, offset, which):
                xr = xt[:, (slot.n + offset) % TPB, :]
                base = steps.before(stage, slot)
                for k in range(NQ):
                    part = xr[:, k * Q:(k + 1) * Q]
                    wbank.wait_filled(dve, stage, slot, k)
                    nc.vector.tensor_tensor(part, wbank.bank(stage, slot, k)[:], part, ALU.add
                                            ).then_inc(wbank.sem(stage, slot, k), 1)
                    wbank.wait_read(dve, stage, slot, k)
                    nc.vector.bn_stats(st6[:, which, k, :], part).then_inc(steps.sem, 1)
                dve.wait_ge(steps.sem, base + NQ)
                nc.vector.memset(fence[:], 0.0)
                nc.vector.bn_aggr(mv[:, which, :], st6[:, which, :, :]).then_inc(stats_ready.sem, 1)

            def ctx_scale(b, p):
                dve.wait_ge(csums_ready, b * DC + DC)
                nc.vector.tensor_reduce(cbound[:], csums[:], AX_X, ALU.max).then_inc(cbound_ready, 1)
                dve.wait_ge(gbound_ready, b + 1)
                nc.vector.tensor_scalar(cpow2[:].bitcast(U32), gbound[:].bitcast(U32), 0x7F800000, None,
                                        ALU.bitwise_and).then_inc(cscale_steps, 1)
                dve.wait_ge(cscale_steps, b * 3 + 1)
                nc.vector.tensor_scalar(cpow2c[:], cpow2[:], 2.0 ** -100, None, ALU.max).then_inc(cscale_steps, 1)
                dve.wait_ge(cscale_steps, b * 3 + 2)
                nc.vector.reciprocal(crpow2[:], cpow2c[:]).then_inc(cscale_steps, 1)
                nc.vector.tensor_scalar(unscore[:, p:p + 1], cpow2c[:], 1.0 / (CTOP * XS), None, ALU.mult)
                nc.vector.tensor_scalar(unexp[:, p:p + 1], cpow2c[:], 1.0 / (CTOP * PS), None, ALU.mult)
                dve.wait_ge(cscale_steps, b * 3 + 3)
                nc.vector.tensor_scalar(cscale[:, p:p + 1], crpow2[:], CTOP, None, ALU.mult).then_inc(cscale_ready, 1)

            def split_cols(b, p, blocks):
                for c in blocks:
                    split_low(nc, dve, ctxT[p], c, cscale[:, p:p + 1], t_high, t_low, b * DC)

            def split_rows(b, p, blocks):
                for c in blocks:
                    split_low(nc, dve, ctxN, c, cscale[:, p:p + 1], n_high, n_low, b * DC)

            def stages(slot):
                b, j = batch(slot, TPB)
                p = (slot.n // TPB + 1) % 2
                if here(slot, -1):
                    base = steps.before("down", slot)
                    wbank.wait_filled(dve, "down", slot)
                    nc.vector.tensor_copy(hs[:], wbank.bank("down", slot)[:, 0:E + ER]).then_inc(wbank.sem("down", slot), 1)
                    wbank.wait_read(dve, "down", slot)
                    nc.vector.tensor_reduce(route[:, 0, 0:1], hs[:, 0:E], AX_X, ALU.max).then_inc(steps.sem, 1)
                    dve.wait_ge(steps.sem, base + 1)
                    nc.vector.scalar_tensor_tensor(route[:, 1, :], hs[:, 0:E], route[:, 0, 0:1], order8[:],
                                                   ALU.is_equal, ALU.mult).then_inc(steps.sem, 1)
                    dve.wait_ge(steps.sem, base + 2)
                    nc.vector.tensor_reduce(route[:, 2, 0:1], route[:, 1, :], AX_X, ALU.max).then_inc(steps.sem, 1)
                    dve.wait_ge(steps.sem, base + 3)
                    nc.vector.tensor_scalar(route[:, 3, :], route[:, 1, :], route[:, 2, 0:1], route[:, 0, 0:1],
                                            ALU.is_equal, ALU.mult).then_inc(steps.sem, 1)
                    dve.wait_ge(steps.sem, base + 4)
                    nc.vector.tensor_tensor(wh[:].rearrange("p (e r) -> p e r", e=E),
                                            hs[:, E:].rearrange("p (e r) -> p e r", e=E),
                                            route[:, 3, :].unsqueeze(2).broadcast_to([P, E, R]), ALU.mult
                                            ).then_inc(wh_ready.sem, 1)
                if here(slot, 1):
                    low("expT", slot, expT, 4, scale=PS)
                if here(slot, 0):
                    base = steps.before("num", slot)
                    c = 0
                    for k, n in enumerate(NUM_FILLS):
                        wbank.wait_filled(dve, "num", slot, k)
                        nd = wbank.bank("num", slot, k)[:, 0:n * NUM].rearrange("p (c m) -> p c m", c=n)
                        nc.vector.reciprocal(rden[:, c:c + n, :], nd[:, :, 2 * HD:NUM]).then_inc(steps.sem, 1)
                        dve.wait_ge(steps.sem, base + k + 1)
                        nc.vector.tensor_tensor(work_a[:, c:c + n, :].rearrange("p c (h m) -> p c h m", h=2),
                                                nd[:, :, 0:2 * HD].rearrange("p c (h m) -> p c h m", h=2),
                                                rden[:, c:c + n, :].unsqueeze(3).broadcast_to([P, n, 2, HD]),
                                                ALU.mult).then_inc(wbank.sem("num", slot, k), 1)
                        c += n
                if j == 3 and here(slot, 1):
                    split_cols(b, p, range(T_EARLY, DC))
                if j == 2 and here(slot, -2):
                    split_rows(b - 1, 1 - p, range(N_EARLY))
                if here(slot, -2):
                    par = (slot.n - 2) // TPB % 2
                    tbank.wait_filled(dve, "scores", slot)
                    nc.vector.tensor_reduce(nsmax[:], tbank.bank("scores", slot)[:], AX_X, ALU.max, negate=True
                                            ).then_inc(steps.sem, 1)
                    dve.wait_ge(steps.sem, steps.after("scores", slot))
                    nc.vector.tensor_scalar(sbias[:], nsmax[:], unscore[:, par:par + 1], None, ALU.mult
                                            ).then_inc(smax_ready.sem, 1)
                if here(slot, 0):
                    add_and_stats(slot, "attn1", 0, LN2)
                if here(slot, -2):
                    low("probT", slot, probT, 1, scale=PS)
                if here(slot, 1):
                    par = (slot.n + 1) % 2
                    base = steps.before("kvs", slot)
                    dve.wait_ge(cexp_ready.sem, cexp_ready.after("cexp", slot.back(1)))
                    nc.vector.reciprocal(rcsum[:], csum[:, par:par + 1]).then_inc(steps.sem, 1)
                    dve.wait_ge(steps.sem, base + 1)
                    pb = (slot.n + 1) // TPB % 2
                    nc.vector.tensor_scalar(rkv[:], rcsum[:], unexp[:, pb:pb + 1], None, ALU.mult).then_inc(steps.sem, 1)
                    dve.wait_ge(steps.sem, base + 2)
                    wbank.wait_filled(dve, "kvs", slot)
                    kvb = wbank.bank("kvs", slot)
                    nc.vector.tensor_scalar(kv[0:HD, par, 0:HD], kvb[0:HD, 0:HD], rkv[0:HD], None, ALU.mult)
                    nc.vector.tensor_scalar(kv[HD:P, par, HD:2 * HD], kvb[HD:P, HD:2 * HD], rkv[HD:P], None, ALU.mult
                                            ).then_inc(wbank.sem("kvs", slot), 1)
                if j == 2 and here(slot, -2):
                    split_rows(b - 1, 1 - p, range(N_EARLY, NQ * TPB))
                if here(slot, -1):
                    add_and_stats(slot, "up", -1, LN3)
                if here(slot, 2):
                    dve.wait_ge(c_loaded.sem, c_loaded.after("load", slot))
                    nc.vector.tensor_reduce(ncmax[:], crow[:], AX_X, ALU.max, negate=True).then_inc(cmax_ready.sem, 1)
                if slot.n == -1:
                    dve.wait_ge(ag_loaded, 16)
                    nc.vector.tensor_reduce(wmax[:, tiles:tiles + 1],
                                            ln2T[:].rearrange("p c a -> p (c a)")[:, 0:DC * AG], AX_X, ALU.max,
                                            apply_absolute_value=True).then_inc(ag_scanned, 1)
                if here(slot, 0):
                    dve.wait_ge(scan_loaded.sem, scan_loaded.after("scan", slot))
                    col = slot.n + slot.rounds * per_round
                    nc.vector.tensor_reduce(wmax[:, bass.ds(col, 1)],
                                            ln2T[:].rearrange("p c a -> p (c a)")[:, 0:share], AX_X, ALU.max,
                                            apply_absolute_value=True).then_inc(scanned.sem, 1)
                if here(slot, 1):
                    b1, j1 = batch(slot, 1)
                    base = steps.before("ln1", slot)
                    dve.wait_ge(x_loaded[j1], b1 * 16 + 16)
                    for k in range(NQ):
                        nc.vector.bn_stats(st6[:, LN1, k, :], xt[:, j1, k * Q:(k + 1) * Q]).then_inc(steps.sem, 1)
                    dve.wait_ge(steps.sem, base + NQ)
                    nc.vector.memset(fence[:], 0.0)
                    nc.vector.bn_aggr(mv[:, LN1, :], st6[:, LN1, :, :]).then_inc(stats_ready.sem, 1)
                if j == 2 and here(slot, 2):
                    ctx_scale(b, p)
                if here(slot, -2):
                    par = (slot.n - 2) // TPB % 2
                    base = steps.before("pv", slot)
                    xr = xt[:, (slot.n - 2) % TPB, :]
                    tbank.wait_read(dve, "scores", slot)
                    nc.vector.reciprocal(rprob[:], psum_row[:]).then_inc(steps.sem, 1)
                    dve.wait_ge(steps.sem, base + 1)
                    nc.vector.tensor_scalar(rpv[:], rprob[:], unexp[:, par:par + 1], None, ALU.mult
                                            ).then_inc(steps.sem, 1)
                    dve.wait_ge(steps.sem, base + 2)
                    for k in range(NQ):
                        part = xr[:, k * Q:(k + 1) * Q]
                        wbank.wait_filled(dve, "pv", slot, k)
                        nc.vector.scalar_tensor_tensor(part, wbank.bank("pv", slot, k)[:], rpv[:], part, ALU.mult,
                                                       ALU.add).then_inc(wbank.sem("pv", slot, k), 1)
                if here(slot, -1):
                    low("ln3T", slot, ln3T, 4)
                if j == 2 and here(slot, 2):
                    split_cols(b, p, range(T_EARLY))

            nc.vector.memset(kv[:], 0.0).then_inc(kv_blank, 1)
            dve.wait_ge(kv_blank, 1)
            nc.vector.memset(kv[0:HD, :, 2 * HD:2 * HD + 1], 1.0)
            nc.vector.memset(kv[HD:P, :, 2 * HD + 1:NUM], 1.0)
            dve.wait_ge(const_ready, 1)
            for s in range(first, TPB):
                stages(Slot(s))
            with dve.Fori(0, (batches - 2) // 2) as r:
                for s in range(TPB, 3 * TPB):
                    stages(Slot(s, r))
            for s in range(tiles - TPB, tiles + 2):
                stages(Slot(s))

        @block.tensor
        def _(pe):
            pe.wait_ge(const_ready, 1)

            def transposed(ring, stage, slot, src):
                for k in range(4):
                    b = ring.take(pe, stage, slot, k)
                    for m in range(4):
                        last = nc.tensor.transpose(b[:, m * P:(m + 1) * P], src(4 * k + m), ident[:])
                    last.then_inc(ring.filled.sem, 1)

            def stages(slot):
                if here(slot, -1):
                    tbank.wait_read(pe, "ln2T", slot.back(1), 3)
                    if slot.n == 1:
                        pe.wait_ge(const_loaded, 32)
                    b = wbank.take(pe, "down", slot)
                    for c in range(DC):
                        last = nc.tensor.matmul(b[:, 0:E + ER], ln2T[:, c, :], ra_sb[:, c, :],
                                                start=(c == 0), stop=(c == DC - 1))
                    last.then_inc(wbank.filled.sem, 1)
                if here(slot, 1):
                    pe.wait_ge(cexp_ready.sem, cexp_ready.after("cexp", slot.back(1)))
                    transposed(tbank, "expT", slot, lambda c: crow[:, c * P:(c + 1) * P])
                if here(slot, 0):
                    pe.wait_ge(q_ready.sem, q_ready.after("q", slot.back(1)))
                    wbank.wait_read(pe, "kvs", slot.back(1))
                    c = 0
                    for k, n in enumerate(NUM_FILLS):
                        b = wbank.take(pe, "num", slot, k)
                        for m in range(n):
                            last = nc.tensor.matmul(b[:, m * NUM:(m + 1) * NUM], work_b[:, c * P:(c + 1) * P],
                                                    kv[:, slot.n % 2, :], start=True, stop=True)
                            c += 1
                        last.then_inc(wbank.filled.sem, 1)
                if here(slot, -2):
                    par = (slot.n - 2) // TPB % 2
                    tbank.wait_read(pe, "ln3T", slot.back(1), 3)
                    b = tbank.take(pe, "scores", slot)
                    split_product(nc, b[:], lambda h, c: ln3T[:, h, c, :],
                                  ctxT[par].half, DC
                                  ).then_inc(tbank.filled.sem, 1)
                if here(slot, 0):
                    wbank.wait_read(pe, "num", slot, len(NUM_FILLS) - 1)
                    transposed(wbank, "attn1", slot, lambda c: work_a[:, c, :])
                if here(slot, -1):
                    pe.wait_ge(wh_ready.sem, wh_ready.after("down", slot))
                    b = tbank.take(pe, "whT", slot)
                    nc.tensor.transpose(b[:, 0:P], wh[:], ident[:]).then_inc(tbank.filled.sem, 1)
                if here(slot, 1):
                    b1, j1 = batch(slot, 1)
                    par = (slot.n + 1) // TPB % 2
                    tbank.wait_read(pe, "expT", slot, 3)
                    if j1 == 0:
                        pe.wait_ge(t_low, b1 * DC + DC)
                    b = wbank.take(pe, "kvs", slot)
                    split_product(nc, b[:, 0:P], lambda h, c: expT[:, h, c, :],
                                  lambda h, c: ctxT[par].half(h, c)[:, j1 * P:(j1 + 1) * P], DC
                                  ).then_inc(wbank.filled.sem, 1)
                if here(slot, -2):
                    tbank.wait_read(pe, "scores", slot)
                    b = tbank.take(pe, "probT", slot)
                    for m in range(TPB):
                        last = nc.tensor.transpose(b[:, m * P:(m + 1) * P], prob[:, m * P:(m + 1) * P], ident[:])
                    last.then_inc(tbank.filled.sem, 1)
                if here(slot, -1):
                    tbank.wait_read(pe, "whT", slot)
                    for k in range(NQ):
                        b = wbank.take(pe, "up", slot, k)
                        nc.tensor.matmul(b[:], whT[:], bwt_sb[:, k * Q:(k + 1) * Q], start=True, stop=True
                                         ).then_inc(wbank.filled.sem, 1)
                if here(slot, -2):
                    b2, j2 = batch(slot, -2)
                    tbank.wait_read(pe, "probT", slot)
                    for k in range(NQ):
                        if j2 == 0:
                            pe.wait_ge(n_low, b2 * DC + TPB * (k + 1))
                        b = wbank.take(pe, "pv", slot, k)
                        split_product(nc, b[:], lambda h, m: probT[:, h, m, :],
                                      lambda h, m: ctxN.half(h, TPB * k + m), TPB
                                      ).then_inc(wbank.filled.sem, 1)
                if here(slot, 0):
                    pe.wait_ge(ln2_ready.sem, ln2_ready.after("ln2", slot))
                    transposed(tbank, "ln2T", slot, lambda c: work_a[:, c, :])
                if here(slot, -1):
                    pe.wait_ge(ln3_ready.sem, ln3_ready.after("ln3", slot))
                    transposed(tbank, "ln3T", slot, lambda c: work_b[:, c * P:(c + 1) * P])

            for s in range(first, TPB):
                stages(Slot(s))
            with pe.Fori(0, (batches - 2) // 2) as r:
                for s in range(TPB, 3 * TPB):
                    stages(Slot(s, r))
            for s in range(tiles - TPB, tiles + 2):
                stages(Slot(s))


def pass_b(nc, ctx, x3, w, ag, wmax, gate_b, b_up, bias, out):
    tiles = x3.shape[0] // P
    per_round = 4
    first = -2

    def sb(name, shape, dt=F32):
        return ctx.enter_context(nc.sbuf_tensor(name, shape, dt))

    def sem(name):
        return ctx.enter_context(nc.semaphore(name))

    wt = InPlace(sb("wt", [P] + InPlace.shape(NQ * DC), F16))
    xt = sb("xt_b", [P, 4, D])
    ln = sb("ln", [P, D])
    lnT = sb("lnT", [P, 2, 2, DC, P], F16)
    ag_sb = sb("ag_sb", [P, 2, DC, AG], F16)
    up_sb = sb("up_sb", [MAXR + 1, D])
    ident = sb("ident_b", [P, P])
    order4 = sb("order4", [P, NG])
    least = sb("least", [P, MAXR])
    gb_sb = sb("gb_sb", [P, NG])
    consts = sb("consts_b", [P, 4])
    tmax = sb("tmax", [P, 2])
    gmax = sb("gmax", [P, 2])
    pow2 = sb("pow2", [P, 2])
    pow2c = sb("pow2c", [P, 2])
    rpow2 = sb("rpow2", [P, 2])
    scale = sb("scale", [P, 2])
    unscale = sb("unscale", [P, 2])
    hm_scale = sb("hm_scale", [P, 1])
    st6 = sb("st6_b", [P, NQ, 6])
    mv = sb("mv_b", [P, 2])
    veps = sb("veps_b", [P, 1])
    rstd1 = sb("rstd1", [P, 1])
    rstd = sb("rstd_b", [P, 1])
    shift1 = sb("shift1_b", [P, 1])
    shift = sb("shift_b", [P, 1])
    fence = sb("fence_b", [P, 1])
    hs = sb("hs_b", [P, AG])
    gate = sb("gate", [P, 3, NG])
    small = sb("small", [P, 8])
    mask = sb("mask", [P, MAXR])
    hm = sb("hm", [P, MAXR + 1])
    hmT = sb("hmT", [MAXR + 1, P])
    def counted(name, stages):
        return Counted(sem(name), stages, tiles, per_round, first)

    T_STAGES = [("hmT", 1, 0), ("lnT", 4, 1)]
    W_STAGES = [("down", 1, 0), ("main", 4, 0)]
    tbank = Banks(nc, ctx, "bt", counted("bt_filled", T_STAGES))
    wbank = Banks(nc, ctx, "bw", counted("bw_filled", W_STAGES))
    high_ready = counted("high_ready", [("lnT", 4, 1)])
    steps = counted("bsteps", [("gate", 12, 0), ("ln", NQ, 1)])
    stats_ready = counted("bstats_ready", [("ln", 1, 1)])
    pool_steps = counted("bpool_steps", [("ln", 3, 1)])
    rstd_ready = counted("brstd_ready", [("ln", 1, 1)])
    ln_ready = counted("ln_ready", [("ln", 1, 1)])
    gexp_ready = counted("gexp_ready", [("gate", 1, 0)])
    x_loaded = [sem(f"bx_loaded{j}") for j in range(4)]
    x_stored = [sem(f"bx_stored{j}") for j in range(4)]
    w_loaded = [sem(f"w_loaded{j}") for j in range(4)]
    ag_loaded = sem("ag_loaded")
    const_loaded = sem("bconst_loaded")
    const_ready = sem("bconst_ready")
    ident_blank = sem("bident_blank")
    tmax_ready = sem("tmax_ready")
    gmax_ready = sem("gmax_ready")
    scale_steps = sem("scale_steps")
    high_split = sem("high_split")
    low_split = sem("low_split")

    def here(slot, offset):
        return 0 <= slot.n + offset < tiles

    def tile(slot, offset):
        return slot.n + offset + per_round * slot.rounds

    def schedule(eng, stages):
        for s in range(first, 4):
            stages(Slot(s))
        with eng.Fori(0, tiles // 4 - 2) as r:
            for s in range(4, 8):
                stages(Slot(s, r))
        for s in range(tiles - 4, tiles):
            stages(Slot(s))

    with nc.Block() as block:

        @block.sync
        def _(sp):
            sp.dma_start(ln[:, 0:DC * AG], ag.rearrange("p c a -> p (c a)")).then_inc(ag_loaded, 16)
            sp.dma_start(xt[:, 0, :], x3[0:P, :]).then_inc(x_loaded[0], 16)
            for g in range(NQ * DC // 4):
                q, c = divmod(4 * g, DC)
                if g >= 4:
                    sp.wait_ge(w_loaded[g % 4], 16 * (g // 4))
                sp.dma_start(wt.raw(4 * g, 4),
                             w[c * P:(c + 4) * P, q * Q:(q + 1) * Q].rearrange("(a p) n -> p a n", p=P)
                             ).then_inc(w_loaded[g % 4], 16)
                if g == 0:
                    sp.dma_start(xt[:, 1, :], x3[P:2 * P, :]).then_inc(x_loaded[1], 16)
            sp.dma_start(up_sb[0:MAXR, :], b_up).then_inc(const_loaded, 16)
            sp.dma_start(up_sb[MAXR:MAXR + 1, :], bias).then_inc(const_loaded, 16)
            sp.dma_start(gb_sb[:], gate_b).then_inc(const_loaded, 16)

            def stages(slot):
                if here(slot, 2) and slot.n >= 0:
                    j = (slot.n + 2) % 4
                    if here(slot, -2):
                        sp.wait_ge(x_stored[j], 16 * ((slot.n + 2) // 4 + slot.rounds))
                    sp.dma_start(xt[:, j, :], x3[bass.ds(tile(slot, 2) * P, P), :]).then_inc(x_loaded[j], 16)
                if here(slot, 0):
                    wbank.wait_read(sp, "main", slot, NQ - 1)
                    sp.dma_start(out[bass.ds(tile(slot, 0) * P, P), :], xt[:, slot.n % 4, :]
                                 ).then_inc(x_stored[slot.n % 4], 16)

            schedule(sp, stages)
            for j in range(4):
                sp.wait_ge(x_stored[j], 16 * (tiles // 4))

        @block.gpsimd
        def _(pool):
            nc.gpsimd.memset(ident[:], 0.0).then_inc(ident_blank, 1)
            for n, value in enumerate((EPS, -0.5, -1.0, XS)):
                nc.gpsimd.memset(consts[:, n:n + 1], value)
            for g in range(NG):
                nc.gpsimd.memset(order4[:, g:g + 1], float(NG - g))
                low = 0 if g == 0 else RANKS[g - 1]
                nc.gpsimd.memset(least[:, low:RANKS[g]], float(NG - g))
            pool.wait_ge(ident_blank, 1)
            nc.gpsimd.affine_select(out=ident[:], in_=ident[:], compare_op=ALU.not_equal, fill=1.0, base=0,
                                    pattern=[[-1, P]], channel_multiplier=1).then_inc(const_ready, 1)
            pool.wait_ge(tmax_ready, 2)
            nc.gpsimd.partition_all_reduce(gmax[:], tmax[:], P, bass.bass_isa.ReduceOp.absmax).then_inc(gmax_ready, 1)

            def stages(slot):
                if here(slot, 1):
                    base = pool_steps.before("ln", slot)
                    pool.wait_ge(stats_ready.sem, stats_ready.after("ln", slot))
                    nc.gpsimd.tensor_tensor(shift1[:], mv[:, 0:1], consts[:, 2:3], ALU.mult)
                    nc.gpsimd.tensor_tensor(veps[:], mv[:, 1:2], consts[:, 0:1], ALU.add).then_inc(pool_steps.sem, 1)
                    pool.wait_ge(pool_steps.sem, base + 1)
                    nc.gpsimd.tensor_tensor(rstd1[:], veps[:], consts[:, 1:2], ALU.pow).then_inc(pool_steps.sem, 1)
                    pool.wait_ge(pool_steps.sem, base + 2)
                    nc.gpsimd.tensor_tensor(rstd[:], rstd1[:], consts[:, 3:4], ALU.mult).then_inc(pool_steps.sem, 1)
                    pool.wait_ge(pool_steps.sem, base + 3)
                    nc.gpsimd.tensor_tensor(shift[:], shift1[:], rstd[:], ALU.mult).then_inc(rstd_ready.sem, 1)

            schedule(pool, stages)

        @block.scalar
        def _(act):
            act.wait_ge(ag_loaded, 16)
            act.wait_ge(scale_steps, 4)
            nc.scalar.activation(ag_sb[:, 0].rearrange("p c a -> p (c a)"), ln[:, 0:DC * AG], ACT.Copy,
                                 scale=scale[:, 1:2]).then_inc(high_split, 1)

            def split_w(q):
                for c in range(q * DC, (q + 1) * DC):
                    if c % 4 == 0:
                        act.wait_ge(w_loaded[c // 4 % 4], 16 * (c // 16 + 1))
                    split_high(nc, act, wt, c, scale[:, 0:1], high_split, low_split, 1)

            def stages(slot):
                if slot.n == 0 and not slot.rounds:
                    for q in range(NQ):
                        split_w(q)
                if here(slot, 0):
                    act.wait_ge(steps.sem, steps.after("gate", slot, 2))
                    nc.scalar.activation(gate[:, 1, :], gate[:, 0, :], ACT.Exp, bias=small[:, 0:1],
                                         accum_out=small[:, 1:2]).then_inc(gexp_ready.sem, 1)
                if here(slot, 1):
                    if slot.n == -1:
                        act.wait_ge(low_split, 1)
                    else:
                        tbank.wait_filled(act, "lnT", slot.back(1), 3)
                    act.wait_ge(rstd_ready.sem, rstd_ready.after("ln", slot))
                    nc.scalar.activation(ln[:], xt[:, (slot.n + 1) % 4, :], ACT.Identity, scale=rstd[:], bias=shift[:]
                                         ).then_inc(ln_ready.sem, 1)
                    for k in range(4):
                        tbank.wait_filled(act, "lnT", slot, k)
                        b = tbank.bank("lnT", slot, k)
                        nc.scalar.activation(
                            lnT[:, (slot.n + 1) % 2, 0, 4 * k:4 * k + 4, :].rearrange("p a b -> p (a b)"), b[:], ACT.Copy
                        ).then_inc(high_ready.sem, 1)

            schedule(act, stages)

        @block.vector
        def _(dve):
            nc.vector.tensor_copy(tmax[:, 1:2], wmax[:, tiles:tiles + 1]).then_inc(tmax_ready, 1)
            nc.vector.tensor_reduce(tmax[:, 0:1], wmax[:, 0:tiles], AX_X, ALU.max).then_inc(tmax_ready, 1)
            dve.wait_ge(gmax_ready, 1)
            nc.vector.tensor_scalar(pow2[:].bitcast(U32), gmax[:].bitcast(U32), 0x7F800000, None, ALU.bitwise_and
                                    ).then_inc(scale_steps, 1)
            dve.wait_ge(scale_steps, 1)
            nc.vector.tensor_scalar(pow2c[:], pow2[:], 2.0 ** -100, None, ALU.max).then_inc(scale_steps, 1)
            dve.wait_ge(scale_steps, 2)
            nc.vector.reciprocal(rpow2[:], pow2c[:]).then_inc(scale_steps, 1)
            nc.vector.tensor_scalar(unscale[:], pow2c[:], 1.0 / (TOP * XS), None, ALU.mult)
            dve.wait_ge(scale_steps, 3)
            nc.vector.tensor_scalar(scale[:], rpow2[:], TOP, None, ALU.mult).then_inc(scale_steps, 1)
            dve.wait_ge(scale_steps, 4)
            nc.vector.tensor_scalar(hm_scale[:], scale[:, 0:1], XS, None, ALU.mult).then_inc(scale_steps, 1)
            nc.vector.tensor_scalar(hm[:, MAXR:MAXR + 1], scale[:, 0:1], XS, None, ALU.mult).then_inc(scale_steps, 1)
            dve.wait_ge(scale_steps, 6)
            dve.wait_ge(high_split, 1)
            nc.vector.scalar_tensor_tensor(ag_sb[:, 1].rearrange("p c a -> p (c a)"), ln[:, 0:DC * AG], scale[:, 1:2],
                                           ag_sb[:, 0].rearrange("p c a -> p (c a)"), ALU.mult, ALU.subtract
                                           ).then_inc(low_split, 1)
            dve.wait_ge(const_ready, 1)

            def split_w(q):
                for c in range(q * DC, (q + 1) * DC):
                    split_low(nc, dve, wt, c, scale[:, 0:1], high_split, low_split, 1)

            def main(slot, k):
                part = xt[:, slot.n % 4, k * Q:(k + 1) * Q]
                wbank.wait_filled(dve, "main", slot, k)
                nc.vector.scalar_tensor_tensor(part, wbank.bank("main", slot, k)[:], unscale[:, 0:1], part, ALU.mult,
                                               ALU.add).then_inc(wbank.sem("main", slot, k), 1)

            def stages(slot):
                if slot.n == 0 and not slot.rounds:
                    dve.wait_ge(const_loaded, 48)
                    for q in range(NQ):
                        split_w(q)
                if here(slot, 0):
                    base = steps.before("gate", slot)
                    done = 0

                    def step(ins):
                        nonlocal done
                        done += 1
                        ins.then_inc(steps.sem, 1)
                        dve.wait_ge(steps.sem, base + done)

                    wbank.wait_filled(dve, "down", slot)
                    nc.vector.tensor_scalar(hs[:], wbank.bank("down", slot)[:, 0:AG], unscale[:, 1:2], None, ALU.mult
                                            ).then_inc(wbank.sem("down", slot), 1)
                    wbank.wait_read(dve, "down", slot)
                    step(nc.vector.tensor_tensor(gate[:, 0, :], hs[:, MAXR:], gb_sb[:], ALU.add))
                    step(nc.vector.tensor_reduce(small[:, 0:1], gate[:, 0, :], AX_X, ALU.max, negate=True))
                    dve.wait_ge(gexp_ready.sem, gexp_ready.after("gate", slot))
                    step(nc.vector.reciprocal(small[:, 2:3], small[:, 1:2]))
                    step(nc.vector.tensor_scalar(gate[:, 0, :], gate[:, 1, :], small[:, 2:3], None, ALU.mult))
                    step(nc.vector.tensor_reduce(small[:, 3:4], gate[:, 0, :], AX_X, ALU.max))
                    step(nc.vector.scalar_tensor_tensor(gate[:, 2, :], gate[:, 0, :], small[:, 3:4], order4[:],
                                                        ALU.is_equal, ALU.mult))
                    step(nc.vector.reciprocal(small[:, 4:5], small[:, 3:4]))
                    step(nc.vector.tensor_tensor(small[:, 5:6], small[:, 3:4], small[:, 4:5], ALU.mult))
                    step(nc.vector.tensor_reduce(small[:, 6:7], gate[:, 2, :], AX_X, ALU.max))
                    step(nc.vector.tensor_scalar(mask[:], least[:], small[:, 6:7], small[:, 5:6], ALU.is_ge, ALU.mult))
                    step(nc.vector.tensor_scalar(hs[:, 0:MAXR], hs[:, 0:MAXR], hm_scale[:], None, ALU.mult))
                    step(nc.vector.tensor_tensor(hm[:, 0:MAXR], hs[:, 0:MAXR], mask[:], ALU.mult))
                if here(slot, 1):
                    j1 = (slot.n + 1) % 4
                    base = steps.before("ln", slot)
                    dve.wait_ge(x_loaded[j1], 16 * ((slot.n + 1) // 4 + slot.rounds) + 16)
                    for k in range(NQ):
                        nc.vector.bn_stats(st6[:, k, :], xt[:, j1, k * Q:(k + 1) * Q]).then_inc(steps.sem, 1)
                    dve.wait_ge(steps.sem, base + NQ)
                    nc.vector.memset(fence[:], 0.0)
                    nc.vector.bn_aggr(mv[:], st6[:]).then_inc(stats_ready.sem, 1)
                if here(slot, 0):
                    tbank.wait_filled(dve, "hmT", slot)
                    nc.vector.tensor_copy(hmT[:], tbank.bank("hmT", slot)[0:MAXR + 1, 0:P]
                                          ).then_inc(tbank.sem("hmT", slot), 1)
                    for k in range(3):
                        main(slot, k)
                if here(slot, 1):
                    for k in range(4):
                        dve.wait_ge(high_ready.sem, high_ready.after("lnT", slot, k + 1))
                        two = [lnT[:, (slot.n + 1) % 2, h, 4 * k:4 * k + 4, :].rearrange("p a b -> p (a b)")
                               for h in range(2)]
                        nc.vector.tensor_tensor(two[1], tbank.bank("lnT", slot, k)[:], two[0], ALU.subtract
                                                ).then_inc(tbank.sem("lnT", slot, k), 1)
                if here(slot, 0):
                    main(slot, 3)

            schedule(dve, stages)

        @block.tensor
        def _(pe):
            pe.wait_ge(const_ready, 1)

            def main(slot, k):
                if slot.n == 0 and not slot.rounds:
                    pe.wait_ge(low_split, 1 + (k + 1) * DC)
                b = wbank.take(pe, "main", slot, k)
                split_product(nc, b[:], lambda h, c: lnT[:, slot.n % 2, h, c, :],
                              lambda h, c: wt.half(h, k * DC + c), DC, stop=False)
                return b

            def lora_up(b, k):
                nc.tensor.matmul(b[:], hmT[:], up_sb[:, k * Q:(k + 1) * Q], start=False, stop=True
                                 ).then_inc(wbank.filled.sem, 1)

            def stages(slot):
                if here(slot, 0):
                    tbank.wait_read(pe, "lnT", slot.back(1), 3)
                    b = wbank.take(pe, "down", slot)
                    split_product(nc, b[:, 0:AG], lambda h, c: lnT[:, slot.n % 2, h, c, :],
                                  lambda h, c: ag_sb[:, h, c, :], DC).then_inc(wbank.filled.sem, 1)
                    b0 = main(slot, 0)
                    pe.wait_ge(steps.sem, steps.after("gate", slot))
                    t = tbank.take(pe, "hmT", slot)
                    nc.tensor.transpose(t[0:MAXR + 1, 0:P], hm[:], ident[:]).then_inc(tbank.filled.sem, 1)
                    b1 = main(slot, 1)
                    tbank.wait_read(pe, "hmT", slot)
                    if slot.n == 0 and not slot.rounds:
                        pe.wait_ge(const_loaded, 48)
                    lora_up(b0, 0)
                    lora_up(b1, 1)
                    lora_up(main(slot, 2), 2)
                if here(slot, 1):
                    pe.wait_ge(ln_ready.sem, ln_ready.after("ln", slot))
                    for k in range(4):
                        b = tbank.take(pe, "lnT", slot, k)
                        for m in range(4):
                            c = 4 * k + m
                            last = nc.tensor.transpose(b[:, m * P:(m + 1) * P], ln[:, c * P:(c + 1) * P], ident[:])
                        last.then_inc(tbank.filled.sem, 1)
                if here(slot, 0):
                    lora_up(main(slot, 3), 3)

            schedule(pe, stages)


def program(nc, x, c_rows, c_cols, ra, bwt, w, ag, gate_b, b_up, bias, out):
    x3 = nc.dram_tensor("x3", x.shape, F32, kind="Internal").ap()
    tiles = x.shape[0] // P
    with nc.sbuf_tensor("wmax", [P, tiles + 1], F32) as wmax:
        with ExitStack() as ctx:
            pass_a(nc, ctx, x, c_rows, c_cols, ra, bwt, w, ag, wmax, x3)
        with ExitStack() as ctx:
            pass_b(nc, ctx, x3, w, ag, wmax, gate_b, b_up, bias, out)


def kernel(x, ctx_4096, L0_ffn_route_w, L0_ffn_A, L0_ffn_Bw, L1_ffn_W, L1_ffn_b, L1_ffn_A, L1_ffn_B,
           L1_ffn_gate_w, L1_ffn_gate_b):
    import numpy as np
    from concourse import bacc
    from concourse.bass_utils import run_bass_kernel_spmd

    shape = x.shape
    batches = shape[0]
    rows = batches * ROWS
    c = np.asarray(ctx_4096)

    def blocks(a):
        return np.ascontiguousarray(a.T.reshape(DC, P, a.shape[0]).transpose(1, 0, 2))

    arrays = {
        "x": np.ascontiguousarray(np.asarray(x).reshape(rows, D)),
        "c_rows": np.ascontiguousarray(c.reshape(rows, D)),
        "c_cols": np.ascontiguousarray(c.reshape(batches, ROWS, DC, P).transpose(0, 3, 2, 1).reshape(batches * P, DC, ROWS)),
        "ra": blocks(np.concatenate([np.asarray(L0_ffn_route_w), np.asarray(L0_ffn_A).reshape(ER, D)])),
        "bwt": np.ascontiguousarray(np.asarray(L0_ffn_Bw).transpose(0, 2, 1).reshape(ER, D)),
        "w": np.ascontiguousarray(np.asarray(L1_ffn_W).T),
        "ag": blocks(np.concatenate([np.asarray(L1_ffn_A), np.asarray(L1_ffn_gate_w)])),
        "gate_b": np.ascontiguousarray(np.broadcast_to(np.asarray(L1_ffn_gate_b), (P, NG))),
        "b_up": np.ascontiguousarray(np.asarray(L1_ffn_B).T),
        "bias": np.ascontiguousarray(np.asarray(L1_ffn_b).reshape(1, D)),
    }
    nc = bacc.Bacc("TRN2", target_bir_lowering=False, num_devices=1)
    aps = {n: nc.dram_tensor(n, a.shape, F32, kind="ExternalInput").ap() for n, a in arrays.items()}
    out = nc.dram_tensor("out", (rows, D), F32, kind="ExternalOutput").ap()
    program(nc, **aps, out=out)
    result = run_bass_kernel_spmd(nc, [arrays], core_ids=[0])
    return result.results[0]["out"].reshape(shape)
```

```python
from contextlib import ExitStack

import concourse.bass as bass
from concourse import mybir

F32 = mybir.dt.float32
F16 = mybir.dt.float16
BF16 = mybir.dt.bfloat16
U32 = mybir.dt.uint32
ALU = mybir.AluOpType
ACT = mybir.ActivationFunctionType
AX_X = mybir.AxisListType.X

P = 128
D = 2048
DC = D // P
ROWS = 512
TPB = ROWS // P
HD = 64
Q = 512
NQ = D // Q
E = 8
R = 16
ER = E * R
EPS = 1e-5
RING = 4
NUM = 2 * HD + 2
NUM_FILLS = [3, 3, 3, 3, 3, 1]
MAXR = 64
NG = 4
RANKS = (8, 16, 32, 64)
AG = MAXR + NG
CTOP = 2.0 ** 14
PS = 4096.0
BIAS_ROW = 2.0 ** 14
XS = 64.0
TOP = 4096.0


class Slot:

    def __init__(self, n, rounds=0):
        self.n, self.rounds = n, rounds

    def back(self, k):
        return Slot(self.n - k, self.rounds)


class Counted:

    def __init__(self, sem, stages, tiles, slots_per_round, first):
        self.sem, self.stages, self.tiles, self.first = sem, stages, tiles, first
        self.per_round = slots_per_round * sum(k for _, k, _ in stages)

    def _count(self, slot, stage, k):
        total = 0
        for s in range(self.first, slot.n + 1):
            for name, raises, offset in self.stages:
                if s == slot.n and name == stage:
                    total += k
                    return total + slot.rounds * self.per_round
                if 0 <= s + offset < self.tiles:
                    total += raises
        raise KeyError(stage)

    def before(self, stage, slot):
        return self._count(slot, stage, 0)

    def after(self, stage, slot, k=None):
        if k is None:
            k = next(r for name, r, _ in self.stages if name == stage)
        return self._count(slot, stage, k)


class Banks:

    def __init__(self, nc, ctx, name, filled):
        self.filled = filled
        self.banks = [ctx.enter_context(nc.psum_tensor(f"{name}_bank{k}", [P, Q], F32)) for k in range(RING)]
        self.emptied = [ctx.enter_context(nc.semaphore(f"{name}_emptied{k}")) for k in range(RING)]

    def _fill(self, stage, slot, k):
        return self.filled.before(stage, Slot(slot.n)) + k

    def bank(self, stage, slot, k=0):
        return self.banks[self._fill(stage, slot, k) % RING]

    def sem(self, stage, slot, k=0):
        return self.emptied[self._fill(stage, slot, k) % RING]

    def wait_filled(self, eng, stage, slot, k=0):
        eng.wait_ge(self.filled.sem, self.filled.after(stage, slot, k + 1))

    def wait_read(self, eng, stage, slot, k=0):
        fill = self._fill(stage, slot, k)
        eng.wait_ge(self.emptied[fill % RING], fill // RING + 1 + slot.rounds * (self.filled.per_round // RING))

    def take(self, eng, stage, slot, k=0):
        fill = self._fill(stage, slot, k)
        if fill >= RING:
            eng.wait_ge(self.emptied[fill % RING], fill // RING + slot.rounds * (self.filled.per_round // RING))
        return self.banks[fill % RING]


class InPlace:

    def __init__(self, units):
        self.units = units

    @staticmethod
    def shape(blocks):
        return [2 * blocks + 2, Q]

    def raw(self, c, n=1):
        return self.units[:, 2 * c + 2:2 * (c + n) + 2, :].rearrange("p (c h) m -> p c (h m)", h=2).bitcast(F32)

    def half(self, h, c):
        return self.units[:, 2 * c + 2 if h else max(2 * c - 1, 0), :]


def split_high(nc, act, buf, c, scale, high_done, low_done, done):
    if c >= 2:
        act.wait_ge(low_done, done + c - 1)
    elif c == 0:
        wait(act, low_done, done)
    nc.scalar.activation(buf.half(0, c), buf.raw(c)[:, 0, :], ACT.Copy, scale=scale).then_inc(high_done, 1)


def split_low(nc, dve, buf, c, scale, high_done, low_done, done):
    dve.wait_ge(high_done, done + c + 1)
    nc.vector.scalar_tensor_tensor(buf.half(1, c), buf.raw(c)[:, 0, :], scale, buf.half(0, c),
                                   ALU.mult, ALU.subtract).then_inc(low_done, 1)


def split_product(nc, dst, left, right, blocks, stop=True, before=None, done=0):
    for c in range(done, blocks):
        if before:
            before(c)
        for n, (hl, hr) in enumerate(((0, 0), (0, 1), (1, 0))):
            last = nc.tensor.matmul(dst, left(hl, c), right(hr, c), start=(c == 0 and n == 0),
                                    stop=(stop and c == blocks - 1 and n == 2))
    return last


def wait(eng, sem, value):
    if isinstance(value, int) and value <= 0:
        return
    eng.wait_ge(sem, value)


class Shared:

    def __init__(self, nc, ctx, tiles):
        def sb(name, shape, dt=F32):
            return ctx.enter_context(nc.sbuf_tensor(name, shape, dt))

        self.w0 = InPlace(sb("w0", [P] + InPlace.shape(DC), F16))
        self.xt = sb("xt", [P, TPB, D])
        self.ident = sb("ident", [P, P])
        self.consts = sb("consts", [P, 4])
        self.wmax = sb("wmax", [P, tiles + 1])
        self.scale = sb("scale", [P, 2])
        self.unscale = sb("unscale", [P, 2])
        self.h_scale = sb("h_scale", [P, 1])
        self.up_scale = sb("up_scale", [P, 1])
        self.bias_scale = sb("bias_scale", [P, 1])
        self.x_loaded = [ctx.enter_context(nc.semaphore(f"bx_loaded{j}")) for j in range(4)]
        self.ag_loaded = ctx.enter_context(nc.semaphore("bag_loaded"))


def pass_a(nc, ctx, x, c_rows, c_cols, ra, bwt, w, ag, b_up, bias, shared, x3):
    batches = x.shape[0] // ROWS
    tiles = batches * TPB
    share = DC * D // tiles
    cuts = D // share
    per_round = 2 * TPB
    first = -2

    def sb(name, shape, dt=F32):
        return ctx.enter_context(nc.sbuf_tensor(name, shape, dt))

    def sem(name):
        return ctx.enter_context(nc.semaphore(name))

    xt, ident, consts, wmax, scale, unscale = (shared.xt, shared.ident, shared.consts, shared.wmax, shared.scale,
                                               shared.unscale)
    ctxT = [shared.w0, InPlace(sb("ctxT", [P] + InPlace.shape(DC), F16))]
    ctxN = InPlace(sb("ctxN", [P] + InPlace.shape(NQ * TPB), F16))
    crow = sb("crow", [P, D])
    expT = sb("expT", [P, 2, DC, P], F16)
    work_a = sb("work_a", [P, DC, P])
    work_b = sb("work_b", [P, D])
    ln2T = sb("ln2T", [P, DC, P])
    ln3T = sb("ln3T", [P, 2, DC, P], F16)
    ra_sb = sb("ra_sb", [P, DC, E + ER])
    bwt_sb = sb("bwt_sb", [ER, D])
    kv = sb("kv", [P, 2, NUM])
    prob = sb("prob", [P, ROWS])
    probT = sb("probT", [P, 2, TPB, P], F16)
    wh = sb("wh", [P, ER])
    whT = sb("whT", [ER, P])
    hs = sb("hs", [P, E + ER])
    order8 = sb("order8", [P, E])
    csums = sb("csums", [P, DC])
    cbound = sb("cbound", [P, 1])
    gbound = sb("gbound", [P, 1])
    pool_fence = sb("pool_fence", [P, 1])
    cpow2 = sb("cpow2", [P, 1])
    tmax = sb("tmax", [P, 4])
    gmax = sb("gmax", [P, 4])
    pow2 = sb("pow2", [P, 4])
    pow2c = sb("pow2c", [P, 4])
    bound2 = sb("bound2", [P, 2])
    top2 = sb("top2", [P, 2])
    rtop2 = sb("rtop2", [P, 2])
    cpow2c = sb("cpow2c", [P, 1])
    crpow2 = sb("crpow2", [P, 1])
    cscale = sb("cscale", [P, 2])
    unscore = sb("unscore", [P, 2])
    unexp = sb("unexp", [P, 2])
    st6 = sb("st6", [P, 3, NQ, 6])
    mv = sb("mv", [P, 3, 2])
    veps = sb("veps", [P, 3])
    rstd = sb("rstd", [P, 3])
    rstd3 = sb("rstd3", [P, 1])
    shift1 = sb("shift1", [P, 3])
    shift = sb("shift", [P, 3])
    fence = sb("fence", [P, 1])
    rden = sb("rden", [P, DC, 2])
    route = sb("route", [P, 4, E])
    ncmax = sb("ncmax", [P, 1])
    csum = sb("csum", [P, 2])
    rcsum = sb("rcsum", [P, 1])
    nsmax = sb("nsmax", [P, 1])
    sbias = sb("sbias", [P, 1])
    rkv = sb("rkv", [P, 1])
    rpv = sb("rpv", [P, 1])
    psum_row = sb("psum_row", [P, 1])
    rprob = sb("rprob", [P, 1])
    def counted(name, stages):
        return Counted(sem(name), stages, tiles, per_round, first)

    T_STAGES = [("expT", 4, 1), ("scores", 1, -2), ("whT", 1, -1), ("probT", 1, -2), ("ln2T", 4, 0), ("ln3T", 4, -1)]
    W_STAGES = [("down", 1, -1), ("num", 6, 0), ("attn1", 4, 0), ("kvs", 1, 1), ("up", 4, -1), ("pv", 4, -2)]
    tbank = Banks(nc, ctx, "t", counted("t_filled", T_STAGES))
    wbank = Banks(nc, ctx, "w", counted("w_filled", W_STAGES))
    steps = counted("steps", [("down", 4, -1), ("num", 6, 0), ("scores", 1, -2), ("attn1", 4, 0),
                              ("kvs", 2, 1), ("up", 4, -1), ("ln1", 4, 1), ("pv", 2, -2)])
    stats_ready = counted("stats_ready", [("attn1", 1, 0), ("up", 1, -1), ("ln1", 1, 1)])
    pool_steps = counted("pool_steps", [("attn1", 2, 0), ("up", 3, -1), ("ln1", 2, 1)])
    high_ready = counted("t_high", [("expT", 4, 1), ("probT", 1, -2), ("ln3T", 4, -1)])
    scan_loaded = counted("scan_loaded", [("scan", 16, 0)])
    scanned = counted("scanned", [("scan", 1, 0)])
    rstd_ready = counted("rstd_ready", [("attn1", 1, 0), ("up", 1, -1), ("ln1", 1, 1)])
    wh_ready = counted("wh_ready", [("down", 1, -1)])
    smax_ready = counted("smax_ready", [("scores", 1, -2)])
    cmax_ready = counted("cmax_ready", [("cexp", 1, 2)])
    cexp_ready = counted("cexp_ready", [("cexp", 1, 2)])
    q_ready = counted("q_ready", [("q", 1, 1)])
    ln2_ready = counted("ln2_ready", [("ln2", 1, 0)])
    ln3_ready = counted("ln3_ready", [("ln3", 1, -1)])
    c_loaded = counted("c_loaded", [("load", 16, 2)])
    x_loaded = [sem(f"x_loaded{j}") for j in range(TPB)]
    x_stored = [sem(f"x_stored{j}") for j in range(TPB)]
    t_loaded = [sem(f"t_loaded{j}") for j in range(NQ)]
    n_loaded = [sem(f"n_loaded{j}") for j in range(NQ)]
    const_loaded = sem("const_loaded")
    const_ready = sem("const_ready")
    ident_blank = sem("ident_blank")
    csums_ready = sem("csums_ready")
    t_high = sem("ctxT_high")
    t_low = sem("ctxT_low")
    n_high = sem("ctxN_high")
    n_low = sem("ctxN_low")
    cbound_ready = sem("cbound_ready")
    gbound_ready = sem("gbound_ready")
    cscale_steps = sem("cscale_steps")
    cscale_ready = sem("cscale_ready")
    ag_loaded = sem("ag_loaded")
    ag_scanned = sem("ag_scanned")
    tmax_blank = sem("tmax_blank")
    up_loaded = sem("up_loaded")
    tmax_ready = sem("tmax_ready")
    gmax_ready = sem("gmax_ready")
    scale_steps = sem("scale_steps")
    w0_loaded = [sem(f"w0_loaded{k}") for k in range(NQ)]
    w_high = sem("w0_high")
    w_low = sem("w0_low")
    kv_blank = sem("kv_blank")

    LN1, LN2, LN3 = 0, 1, 2
    B_EARLY, T_EARLY, N_EARLY = 8, 6, 12
    W_EARLY = 8

    def batch(slot, offset):
        return (slot.n + offset) // TPB + 2 * slot.rounds, (slot.n + offset) % TPB

    def here(slot, offset):
        return 0 <= slot.n + offset < tiles

    with nc.Block() as block:

        @block.sync
        def _(sp):
            def load_cols(b, parity):
                for k in range(NQ):
                    sp.dma_start(ctxT[parity].raw(4 * k, 4), c_cols[bass.ds(b * P, P), k * 4:k * 4 + 4, :]
                                 ).then_inc(t_loaded[k], 16)

            def load_x(b, j):
                sp.dma_start(xt[:, j, :], x[bass.ds(b * ROWS + j * P, P), :]).then_inc(x_loaded[j], 16)

            def stages(slot):
                if here(slot, 2):
                    b, j = batch(slot, 2)
                    if here(slot, 1):
                        tbank.wait_read(sp, "expT", slot, 3)
                    sp.dma_start(crow[:], c_rows[bass.ds(b * ROWS + j * P, P), :]).then_inc(c_loaded.sem, 16)
                if slot.n == first:
                    load_x(0, 0)
                    load_cols(0, 0)
                    sp.dma_start(ra_sb[:], ra).then_inc(const_loaded, 16)
                    sp.dma_start(bwt_sb[:], bwt).then_inc(const_loaded, 16)
                    sp.dma_start(ln2T[:].rearrange("p c a -> p (c a)")[:, 0:DC * AG], ag.rearrange("p c a -> p (c a)")
                                 ).then_inc(ag_loaded, 16)
                    sp.dma_start(work_a[0:MAXR].rearrange("p a b -> p (a b)"), b_up).then_inc(up_loaded, 16)
                    sp.dma_start(work_a[MAXR:MAXR + 1].rearrange("p a b -> p (a b)"), bias).then_inc(up_loaded, 16)
                    for k in range(NQ):
                        sp.dma_start(ctxN.raw(4 * k, 4),
                                     c_rows[0:ROWS, k * Q:(k + 1) * Q].rearrange("(a p) n -> p a n", p=P)
                                     ).then_inc(n_loaded[k], 16)
                if slot.n == 0:
                    load_cols(1, 1)
                b, j = batch(slot, 0)
                if here(slot, 0):
                    if here(slot, -1):
                        wbank.wait_filled(sp, "down", slot)
                    else:
                        sp.wait_ge(ag_scanned, 1)
                    sp.dma_start(ln2T[:].rearrange("p c a -> p (c a)")[:, 0:share],
                                 w[bass.ds((slot.n // cuts + slot.rounds * (per_round // cuts)) * P, P),
                                   slot.n % cuts * share:(slot.n % cuts + 1) * share]).then_inc(scan_loaded.sem, 16)
                if slot.n >= TPB and j == 1 and here(slot, TPB):
                    tbank.wait_filled(sp, "scores", slot)
                    load_cols(b + 1, (slot.n // TPB + 1) % 2)
                if slot.n >= TPB and j == 1 and here(slot, 0):
                    for k in range(NQ):
                        wbank.wait_filled(sp, "pv", slot, min(k + 1, NQ - 1))
                        sp.dma_start(ctxN.raw(4 * k, 4),
                                     c_rows[bass.ds(b * ROWS, ROWS), k * Q:(k + 1) * Q].rearrange("(a p) n -> p a n", p=P)
                                     ).then_inc(n_loaded[k], 16)
                if here(slot, -2):
                    bs, js = batch(slot, -2)
                    wbank.wait_read(sp, "pv", slot, NQ - 1)
                    sp.dma_start(x3[bass.ds(bs * ROWS + js * P, P), :], xt[:, js, :]).then_inc(x_stored[js], 16)
                if slot.n > first and here(slot, 2):
                    bl, jl = batch(slot, 2)
                    if here(slot, -2):
                        sp.wait_ge(x_stored[jl], bl * 16)
                    load_x(bl, jl)
                if slot.n == tiles - TPB + 1 and not slot.rounds:
                    tbank.wait_filled(sp, "scores", slot)
                    for c in range(0, DC, 4):
                        sp.dma_start(shared.w0.raw(c, 4), w[c * P:(c + 4) * P, 0:Q].rearrange("(a p) n -> p a n", p=P)
                                     ).then_inc(w0_loaded[c // 4], 16)
                j = slot.n - (tiles - 1)
                if j in (0, 1):
                    sp.wait_ge(x_stored[j], batches * 16)
                    sp.dma_start(xt[:, j, :], x3[j * P:(j + 1) * P, :]).then_inc(shared.x_loaded[j], 16)
                if j == 2:
                    sp.wait_ge(x_stored[j], batches * 16)
                    sp.dma_start(xt[:, j, 0:DC * AG], ag.rearrange("p c a -> p (c a)")).then_inc(shared.ag_loaded, 16)

            for s in range(first, TPB):
                stages(Slot(s))
            with sp.Fori(0, (batches - 2) // 2) as r:
                for s in range(TPB, 3 * TPB):
                    stages(Slot(s, r))
            for s in range(tiles - TPB, tiles + 2):
                stages(Slot(s))
            for j in range(TPB):
                sp.wait_ge(x_stored[j], batches * 16)

        @block.gpsimd
        def _(pool):
            nc.gpsimd.memset(ident[:], 0.0).then_inc(ident_blank, 1)
            for n, value in enumerate((EPS, -0.5, -1.0, XS)):
                nc.gpsimd.memset(consts[:, n:n + 1], value)
            for e in range(E):
                nc.gpsimd.memset(order8[:, e:e + 1], float(E - e))
            pool.wait_ge(ident_blank, 1)
            nc.gpsimd.affine_select(out=ident[:], in_=ident[:], compare_op=ALU.not_equal, fill=1.0, base=0,
                                    pattern=[[-1, P]], channel_multiplier=1).then_inc(const_ready, 1)

            def layernorm_scale(slot, stage, which):
                base = pool_steps.before(stage, slot)
                one = slice(which, which + 1)
                pool.wait_ge(stats_ready.sem, stats_ready.after(stage, slot))
                nc.gpsimd.tensor_tensor(shift1[:, one], mv[:, which, 0:1], consts[:, 2:3], ALU.mult)
                nc.gpsimd.tensor_tensor(veps[:, one], mv[:, which, 1:2], consts[:, 0:1], ALU.add
                                        ).then_inc(pool_steps.sem, 1)
                pool.wait_ge(pool_steps.sem, base + 1)
                power = rstd3[:] if which == LN3 else rstd[:, one]
                nc.gpsimd.tensor_tensor(power, veps[:, one], consts[:, 1:2], ALU.pow).then_inc(pool_steps.sem, 1)
                pool.wait_ge(pool_steps.sem, base + 2)
                if which == LN3:
                    nc.gpsimd.tensor_tensor(rstd[:, one], power, consts[:, 3:4], ALU.mult).then_inc(pool_steps.sem, 1)
                    pool.wait_ge(pool_steps.sem, base + 3)
                nc.gpsimd.tensor_tensor(shift[:, one], shift1[:, one], rstd[:, one], ALU.mult
                                        ).then_inc(rstd_ready.sem, 1)

            def stages(slot):
                if here(slot, 0):
                    layernorm_scale(slot, "attn1", LN2)
                b, j = batch(slot, TPB)
                if j == 2 and here(slot, 2):
                    pool.wait_ge(cbound_ready, b + 1)
                    nc.gpsimd.tensor_tensor(pool_fence[:], consts[:, 0:1], consts[:, 1:2], ALU.mult)
                    nc.gpsimd.partition_all_reduce(gbound[:], cbound[:], P, bass.bass_isa.ReduceOp.absmax
                                                   ).then_inc(gbound_ready, 1)
                if here(slot, -1):
                    layernorm_scale(slot, "up", LN3)
                if here(slot, 1):
                    layernorm_scale(slot, "ln1", LN1)
                if slot.n == tiles:
                    pool.wait_ge(tmax_ready, 4)
                    nc.gpsimd.partition_all_reduce(gmax[:], tmax[:], P, bass.bass_isa.ReduceOp.absmax
                                                   ).then_inc(gmax_ready, 1)

            for s in range(first, TPB):
                stages(Slot(s))
            with pool.Fori(0, (batches - 2) // 2) as r:
                for s in range(TPB, 3 * TPB):
                    stages(Slot(s, r))
            for s in range(tiles - TPB, tiles + 2):
                stages(Slot(s))

        @block.scalar
        def _(act):
            def empty(stage, slot, dst):
                for k in range(4):
                    tbank.wait_filled(act, stage, slot, k)
                    nc.scalar.activation(dst[:, 4 * k:4 * k + 4, :].rearrange("p a b -> p (a b)"),
                                         tbank.bank(stage, slot, k)[:], ACT.Copy).then_inc(tbank.sem(stage, slot, k), 1)

            def high(stage, slot, dst, fills, scale=1.0):
                for k in range(fills):
                    tbank.wait_filled(act, stage, slot, k)
                    nc.scalar.activation(dst[:, 0, 4 * k:4 * k + 4, :].rearrange("p a b -> p (a b)"),
                                         tbank.bank(stage, slot, k)[:], ACT.Copy, scale=scale
                                         ).then_inc(high_ready.sem, 1)

            def bound_cols(b, p, blocks):
                for c in blocks:
                    if c % 4 == 0:
                        act.wait_ge(t_loaded[c // 4], b * 16 + 16)
                    if c > 1:
                        act.wait_ge(csums_ready, b * DC + c - 1)
                    nc.scalar.activation(ctxT[p].units[:, c % 2, :].bitcast(BF16), ctxT[p].raw(c)[:, 0, :], ACT.Abs,
                                         accum_out=csums[:, c:c + 1]).then_inc(csums_ready, 1)

            def split_cols(b, p, blocks):
                act.wait_ge(cscale_ready, b + 1)
                for c in blocks:
                    split_high(nc, act, ctxT[p], c, cscale[:, p:p + 1], t_high, t_low, b * DC)

            def split_rows(b, p, blocks):
                for c in blocks:
                    if c % TPB == 0:
                        act.wait_ge(n_loaded[c // TPB], b * 16 + 16)
                    split_high(nc, act, ctxN, c, cscale[:, p:p + 1], n_high, n_low, b * DC)

            def split_w(blocks):
                for c in blocks:
                    if c % 4 == 0:
                        act.wait_ge(w0_loaded[c // 4], 16)
                    split_high(nc, act, shared.w0, c, scale[:, 0:1], w_high, w_low, 0)

            def stages(slot):
                b, j = batch(slot, TPB)
                p = (slot.n // TPB + 1) % 2
                if slot.n == tiles + 1:
                    split_w(range(W_EARLY, DC))
                if here(slot, 1):
                    high("expT", slot, expT, 4, scale=PS)
                if j == 3 and here(slot, 1):
                    split_cols(b, p, range(T_EARLY, DC))
                if j == 2 and here(slot, -2):
                    split_rows(b - 1, 1 - p, range(N_EARLY))
                if here(slot, 2) and j == 2 and slot.n > 0:
                    bound_cols(b, p, range(B_EARLY, DC))
                if here(slot, -2):
                    act.wait_ge(smax_ready.sem, smax_ready.after("scores", slot))
                    nc.scalar.activation(prob[:], tbank.bank("scores", slot)[:], ACT.Exp, bias=sbias[:],
                                         scale=unscore[:, (slot.n - 2) // TPB % 2:(slot.n - 2) // TPB % 2 + 1],
                                         accum_out=psum_row[:]).then_inc(tbank.sem("scores", slot), 1)
                if here(slot, -1):
                    tbank.wait_filled(act, "whT", slot)
                    nc.scalar.activation(whT[:], tbank.bank("whT", slot)[:, 0:P], ACT.Copy
                                         ).then_inc(tbank.sem("whT", slot), 1)
                if here(slot, -2):
                    high("probT", slot, probT, 1, scale=PS)
                if j == 2 and here(slot, -2):
                    split_rows(b - 1, 1 - p, range(N_EARLY, NQ * TPB))
                if here(slot, 0):
                    act.wait_ge(rstd_ready.sem, rstd_ready.after("attn1", slot))
                    nc.scalar.activation(work_a[:].rearrange("p a b -> p (a b)"), xt[:, slot.n % TPB, :], ACT.Identity,
                                         scale=rstd[:, LN2:LN2 + 1], bias=shift[:, LN2:LN2 + 1]
                                         ).then_inc(ln2_ready.sem, 1)
                if here(slot, TPB) and slot.n > 0 and j == 1:
                    bound_cols(b, p, range(B_EARLY))
                if here(slot, -1):
                    act.wait_ge(rstd_ready.sem, rstd_ready.after("up", slot))
                    nc.scalar.activation(work_b[:], xt[:, (slot.n - 1) % TPB, :], ACT.Identity,
                                         scale=rstd[:, LN3:LN3 + 1], bias=shift[:, LN3:LN3 + 1]
                                         ).then_inc(ln3_ready.sem, 1)
                if here(slot, 2):
                    par = slot.n % 2
                    act.wait_ge(cmax_ready.sem, cmax_ready.after("cexp", slot))
                    nc.scalar.activation(crow[:], crow[:], ACT.Exp, bias=ncmax[:], accum_out=csum[:, par:par + 1]
                                         ).then_inc(cexp_ready.sem, 1)
                if slot.n == first:
                    bound_cols(0, 0, range(DC))
                if here(slot, 0):
                    act.wait_ge(scanned.sem, scanned.after("scan", slot))
                    empty("ln2T", slot, ln2T)
                if here(slot, -1):
                    high("ln3T", slot, ln3T, 4)
                if here(slot, 1):
                    act.wait_ge(rstd_ready.sem, rstd_ready.after("ln1", slot))
                    nc.scalar.activation(work_b[:], xt[:, (slot.n + 1) % TPB, :], ACT.Exp,
                                         scale=rstd[:, LN1:LN1 + 1], bias=shift[:, LN1:LN1 + 1]
                                         ).then_inc(q_ready.sem, 1)
                if j == 2 and here(slot, 2):
                    split_cols(b, p, range(T_EARLY))
                if slot.n == tiles:
                    act.wait_ge(scale_steps, 8)
                    split_w(range(W_EARLY))

            for s in range(first, TPB):
                stages(Slot(s))
            with act.Fori(0, (batches - 2) // 2) as r:
                for s in range(TPB, 3 * TPB):
                    stages(Slot(s, r))
            for s in range(tiles - TPB, tiles + 2):
                stages(Slot(s))

        @block.vector
        def _(dve):
            def low(stage, slot, dst, fills, scale=None):
                for k in range(fills):
                    dve.wait_ge(high_ready.sem, high_ready.after(stage, slot, k + 1))
                    halves = [dst[:, h, 4 * k:4 * k + 4, :].rearrange("p a b -> p (a b)") for h in range(2)]
                    b = tbank.bank(stage, slot, k)[:]
                    if scale is None:
                        ins = nc.vector.tensor_tensor(halves[1], b, halves[0], ALU.subtract)
                    else:
                        ins = nc.vector.scalar_tensor_tensor(halves[1], b, scale, halves[0], ALU.mult, ALU.subtract)
                    ins.then_inc(tbank.sem(stage, slot, k), 1)

            def add_and_stats(slot, stage, offset, which):
                xr = xt[:, (slot.n + offset) % TPB, :]
                base = steps.before(stage, slot)
                for k in range(NQ):
                    part = xr[:, k * Q:(k + 1) * Q]
                    wbank.wait_filled(dve, stage, slot, k)
                    nc.vector.tensor_tensor(part, wbank.bank(stage, slot, k)[:], part, ALU.add
                                            ).then_inc(wbank.sem(stage, slot, k), 1)
                for k in range(NQ):
                    wbank.wait_read(dve, stage, slot, k)
                    nc.vector.bn_stats(st6[:, which, k, :], xr[:, k * Q:(k + 1) * Q]).then_inc(steps.sem, 1)
                dve.wait_ge(steps.sem, base + NQ)
                nc.vector.memset(fence[:], 0.0)
                nc.vector.bn_aggr(mv[:, which, :], st6[:, which, :, :]).then_inc(stats_ready.sem, 1)

            def bound(b):
                dve.wait_ge(csums_ready, b * DC + DC)
                nc.vector.tensor_reduce(cbound[:], csums[:], AX_X, ALU.max).then_inc(cbound_ready, 1)

            def ctx_scale(b, p):
                dve.wait_ge(gbound_ready, b + 1)
                nc.vector.tensor_scalar(cpow2[:].bitcast(U32), gbound[:].bitcast(U32), 0x7F800000, None,
                                        ALU.bitwise_and).then_inc(cscale_steps, 1)
                dve.wait_ge(cscale_steps, b * 3 + 1)
                nc.vector.tensor_scalar(cpow2c[:], cpow2[:], 2.0 ** -100, None, ALU.max).then_inc(cscale_steps, 1)
                dve.wait_ge(cscale_steps, b * 3 + 2)
                nc.vector.reciprocal(crpow2[:], cpow2c[:]).then_inc(cscale_steps, 1)
                nc.vector.tensor_scalar(unscore[:, p:p + 1], cpow2c[:], 1.0 / (CTOP * XS), None, ALU.mult)
                nc.vector.tensor_scalar(unexp[:, p:p + 1], cpow2c[:], 1.0 / (CTOP * PS), None, ALU.mult)
                dve.wait_ge(cscale_steps, b * 3 + 3)
                nc.vector.tensor_scalar(cscale[:, p:p + 1], crpow2[:], CTOP, None, ALU.mult).then_inc(cscale_ready, 1)

            def split_cols(b, p, blocks):
                for c in blocks:
                    split_low(nc, dve, ctxT[p], c, cscale[:, p:p + 1], t_high, t_low, b * DC)

            def split_rows(b, p, blocks):
                for c in blocks:
                    split_low(nc, dve, ctxN, c, cscale[:, p:p + 1], n_high, n_low, b * DC)

            def w_scale():
                dve.wait_ge(gmax_ready, 1)
                done = 0

                def step(ins):
                    nonlocal done
                    done += 1
                    ins.then_inc(scale_steps, 1)
                    dve.wait_ge(scale_steps, done)

                step(nc.vector.tensor_scalar(pow2[:].bitcast(U32), gmax[:].bitcast(U32), 0x7F800000, None,
                                             ALU.bitwise_and))
                step(nc.vector.tensor_scalar(pow2c[:], pow2[:], 2.0 ** -50, None, ALU.max))
                step(nc.vector.scalar_tensor_tensor(bound2[:, 0:1], pow2c[:, 2:3], 8.0, pow2c[:, 1:2], ALU.mult,
                                                    ALU.mult))
                step(nc.vector.scalar_tensor_tensor(bound2[:, 1:2], pow2c[:, 3:4], 2.0 ** -8, pow2c[:, 0:1], ALU.mult,
                                                    ALU.max))
                step(nc.vector.tensor_tensor(top2[:, 0:1], bound2[:, 0:1], bound2[:, 1:2], ALU.max))
                step(nc.vector.tensor_copy(top2[:, 1:2], pow2c[:, 1:2]))
                step(nc.vector.reciprocal(rtop2[:], top2[:]))
                nc.vector.tensor_scalar(unscale[:], top2[:], 1.0 / (TOP * XS), None, ALU.mult)
                nc.vector.tensor_scalar(shared.h_scale[:], rtop2[:, 1:2], 8.0, None, ALU.mult)
                nc.vector.scalar_tensor_tensor(shared.up_scale[:], top2[:, 1:2], XS * TOP / 8.0, rtop2[:, 0:1],
                                               ALU.mult, ALU.mult)
                nc.vector.tensor_scalar(shared.bias_scale[:], rtop2[:, 0:1], XS * TOP / BIAS_ROW, None, ALU.mult)
                step(nc.vector.tensor_scalar(scale[:], rtop2[:], TOP, None, ALU.mult))

            def split_w(blocks):
                for c in blocks:
                    split_low(nc, dve, shared.w0, c, scale[:, 0:1], w_high, w_low, 0)

            def stages(slot):
                b, j = batch(slot, TPB)
                p = (slot.n // TPB + 1) % 2
                if slot.n == tiles + 1:
                    split_w(range(W_EARLY, DC))
                if here(slot, -1):
                    base = steps.before("down", slot)
                    wbank.wait_filled(dve, "down", slot)
                    nc.vector.tensor_copy(hs[:], wbank.bank("down", slot)[:, 0:E + ER]).then_inc(wbank.sem("down", slot), 1)
                    wbank.wait_read(dve, "down", slot)
                    nc.vector.tensor_reduce(route[:, 0, 0:1], hs[:, 0:E], AX_X, ALU.max).then_inc(steps.sem, 1)
                    dve.wait_ge(steps.sem, base + 1)
                    nc.vector.scalar_tensor_tensor(route[:, 1, :], hs[:, 0:E], route[:, 0, 0:1], order8[:],
                                                   ALU.is_equal, ALU.mult).then_inc(steps.sem, 1)
                    dve.wait_ge(steps.sem, base + 2)
                    nc.vector.tensor_reduce(route[:, 2, 0:1], route[:, 1, :], AX_X, ALU.max).then_inc(steps.sem, 1)
                    dve.wait_ge(steps.sem, base + 3)
                    nc.vector.tensor_scalar(route[:, 3, :], route[:, 1, :], route[:, 2, 0:1], route[:, 0, 0:1],
                                            ALU.is_equal, ALU.mult).then_inc(steps.sem, 1)
                    dve.wait_ge(steps.sem, base + 4)
                    nc.vector.tensor_tensor(wh[:].rearrange("p (e r) -> p e r", e=E),
                                            hs[:, E:].rearrange("p (e r) -> p e r", e=E),
                                            route[:, 3, :].unsqueeze(2).broadcast_to([P, E, R]), ALU.mult
                                            ).then_inc(wh_ready.sem, 1)
                if here(slot, 1):
                    low("expT", slot, expT, 4, scale=PS)

                def splits():
                    if j == 3 and here(slot, 1):
                        split_cols(b, p, range(T_EARLY, DC))
                    if j == 2 and here(slot, -2):
                        split_rows(b - 1, 1 - p, range(N_EARLY))

                if not here(slot, 0):
                    splits()
                else:
                    base = steps.before("num", slot)
                    starts = [sum(NUM_FILLS[:k]) for k in range(len(NUM_FILLS))]

                    def num_block(k):
                        n = NUM_FILLS[k]
                        return wbank.bank("num", slot, k)[:, 0:n * NUM].rearrange("p (c m) -> p c m", c=n)

                    def reciprocals(k):
                        wbank.wait_filled(dve, "num", slot, k)
                        nc.vector.reciprocal(rden[:, starts[k]:starts[k] + NUM_FILLS[k], :],
                                             num_block(k)[:, :, 2 * HD:NUM]).then_inc(steps.sem, 1)

                    reciprocals(0)
                    for k, (c, n) in enumerate(zip(starts, NUM_FILLS)):
                        if k == RING - 1:
                            splits()
                        if k + 1 < len(NUM_FILLS):
                            reciprocals(k + 1)
                        dve.wait_ge(steps.sem, base + k + 1)
                        nc.vector.tensor_tensor(work_a[:, c:c + n, :].rearrange("p c (h m) -> p c h m", h=2),
                                                num_block(k)[:, :, 0:2 * HD].rearrange("p c (h m) -> p c h m", h=2),
                                                rden[:, c:c + n, :].unsqueeze(3).broadcast_to([P, n, 2, HD]),
                                                ALU.mult).then_inc(wbank.sem("num", slot, k), 1)
                if here(slot, -2):
                    par = (slot.n - 2) // TPB % 2
                    tbank.wait_filled(dve, "scores", slot)
                    nc.vector.tensor_reduce(nsmax[:], tbank.bank("scores", slot)[:], AX_X, ALU.max, negate=True
                                            ).then_inc(steps.sem, 1)
                    dve.wait_ge(steps.sem, steps.after("scores", slot))
                    nc.vector.tensor_scalar(sbias[:], nsmax[:], unscore[:, par:par + 1], None, ALU.mult
                                            ).then_inc(smax_ready.sem, 1)
                if here(slot, 0):
                    add_and_stats(slot, "attn1", 0, LN2)
                if here(slot, 1):
                    par = (slot.n + 1) % 2
                    base = steps.before("kvs", slot)
                    dve.wait_ge(cexp_ready.sem, cexp_ready.after("cexp", slot.back(1)))
                    nc.vector.reciprocal(rcsum[:], csum[:, par:par + 1]).then_inc(steps.sem, 1)
                    dve.wait_ge(steps.sem, base + 1)
                    pb = (slot.n + 1) // TPB % 2
                    nc.vector.tensor_scalar(rkv[:], rcsum[:], unexp[:, pb:pb + 1], None, ALU.mult).then_inc(steps.sem, 1)
                    dve.wait_ge(steps.sem, base + 2)
                    wbank.wait_filled(dve, "kvs", slot)
                    kvb = wbank.bank("kvs", slot)
                    nc.vector.tensor_scalar(kv[0:HD, par, 0:HD], kvb[0:HD, 0:HD], rkv[0:HD], None, ALU.mult)
                    nc.vector.tensor_scalar(kv[HD:P, par, HD:2 * HD], kvb[HD:P, HD:2 * HD], rkv[HD:P], None, ALU.mult
                                            ).then_inc(wbank.sem("kvs", slot), 1)
                if here(slot, -2):
                    low("probT", slot, probT, 1, scale=PS)
                if j == 2 and here(slot, 2) and slot.n > 0:
                    bound(b)
                if here(slot, -1):
                    add_and_stats(slot, "up", -1, LN3)
                if j == 2 and here(slot, -2):
                    split_rows(b - 1, 1 - p, range(N_EARLY, NQ * TPB))
                if here(slot, 2):
                    dve.wait_ge(c_loaded.sem, c_loaded.after("load", slot))
                    nc.vector.tensor_reduce(ncmax[:], crow[:], AX_X, ALU.max, negate=True).then_inc(cmax_ready.sem, 1)
                if here(slot, 0):
                    dve.wait_ge(scan_loaded.sem, scan_loaded.after("scan", slot))
                    col = slot.n + slot.rounds * per_round
                    nc.vector.tensor_reduce(wmax[:, bass.ds(col, 1)],
                                            ln2T[:].rearrange("p c a -> p (c a)")[:, 0:share], AX_X, ALU.max,
                                            apply_absolute_value=True).then_inc(scanned.sem, 1)
                if here(slot, 1):
                    b1, j1 = batch(slot, 1)
                    base = steps.before("ln1", slot)
                    dve.wait_ge(x_loaded[j1], b1 * 16 + 16)
                    for k in range(NQ):
                        nc.vector.bn_stats(st6[:, LN1, k, :], xt[:, j1, k * Q:(k + 1) * Q]).then_inc(steps.sem, 1)
                    dve.wait_ge(steps.sem, base + NQ)
                    nc.vector.memset(fence[:], 0.0)
                    nc.vector.bn_aggr(mv[:, LN1, :], st6[:, LN1, :, :]).then_inc(stats_ready.sem, 1)
                if slot.n == -1:
                    dve.wait_ge(ag_loaded, 16)
                    nc.vector.tensor_reduce(wmax[:, tiles:tiles + 1],
                                            ln2T[:].rearrange("p c a -> p (c a)")[:, 0:DC * AG], AX_X, ALU.max,
                                            apply_absolute_value=True).then_inc(ag_scanned, 1)
                    dve.wait_ge(up_loaded, 32)
                    dve.wait_ge(tmax_blank, 1)
                    for rows, col in ((slice(0, MAXR), 2), (slice(MAXR, MAXR + 1), 3)):
                        nc.vector.tensor_reduce(tmax[rows, col:col + 1], work_a[rows].rearrange("p a b -> p (a b)"),
                                                AX_X, ALU.max, apply_absolute_value=True).then_inc(tmax_ready, 1)
                if slot.n == first:
                    bound(0)
                if j == 2 and here(slot, 2):
                    ctx_scale(b, p)
                if here(slot, -2):
                    par = (slot.n - 2) // TPB % 2
                    base = steps.before("pv", slot)
                    xr = xt[:, (slot.n - 2) % TPB, :]
                    tbank.wait_read(dve, "scores", slot)
                    nc.vector.reciprocal(rprob[:], psum_row[:]).then_inc(steps.sem, 1)
                    dve.wait_ge(steps.sem, base + 1)
                    nc.vector.tensor_scalar(rpv[:], rprob[:], unexp[:, par:par + 1], None, ALU.mult
                                            ).then_inc(steps.sem, 1)
                    dve.wait_ge(steps.sem, base + 2)
                    for k in range(NQ):
                        part = xr[:, k * Q:(k + 1) * Q]
                        wbank.wait_filled(dve, "pv", slot, k)
                        nc.vector.scalar_tensor_tensor(part, wbank.bank("pv", slot, k)[:], rpv[:], part, ALU.mult,
                                                       ALU.add).then_inc(wbank.sem("pv", slot, k), 1)
                if here(slot, -1):
                    low("ln3T", slot, ln3T, 4)
                if j == 2 and here(slot, 2):
                    split_cols(b, p, range(T_EARLY))
                if slot.n == tiles - 1:
                    dve.wait_ge(scanned.sem, tiles)
                    nc.vector.tensor_copy(tmax[:, 1:2], wmax[:, tiles:tiles + 1]).then_inc(tmax_ready, 1)
                    nc.vector.tensor_reduce(tmax[:, 0:1], wmax[:, 0:tiles], AX_X, ALU.max).then_inc(tmax_ready, 1)
                if slot.n == tiles:
                    w_scale()
                    split_w(range(W_EARLY))

            nc.vector.memset(tmax[:], 0.0).then_inc(tmax_blank, 1)
            nc.vector.memset(kv[:], 0.0).then_inc(kv_blank, 1)
            dve.wait_ge(kv_blank, 1)
            nc.vector.memset(kv[0:HD, :, 2 * HD:2 * HD + 1], 1.0)
            nc.vector.memset(kv[HD:P, :, 2 * HD + 1:NUM], 1.0)
            dve.wait_ge(const_ready, 1)
            for s in range(first, TPB):
                stages(Slot(s))
            with dve.Fori(0, (batches - 2) // 2) as r:
                for s in range(TPB, 3 * TPB):
                    stages(Slot(s, r))
            for s in range(tiles - TPB, tiles + 2):
                stages(Slot(s))

        @block.tensor
        def _(pe):
            pe.wait_ge(const_ready, 1)

            def transposed(ring, stage, slot, src):
                for k in range(4):
                    b = ring.take(pe, stage, slot, k)
                    for m in range(4):
                        last = nc.tensor.transpose(b[:, m * P:(m + 1) * P], src(4 * k + m), ident[:])
                    last.then_inc(ring.filled.sem, 1)

            def stages(slot):
                if here(slot, -1):
                    tbank.wait_read(pe, "ln2T", slot.back(1), 3)
                    if slot.n == 1:
                        pe.wait_ge(const_loaded, 32)
                    b = wbank.take(pe, "down", slot)
                    for c in range(DC):
                        last = nc.tensor.matmul(b[:, 0:E + ER], ln2T[:, c, :], ra_sb[:, c, :],
                                                start=(c == 0), stop=(c == DC - 1))
                    last.then_inc(wbank.filled.sem, 1)
                if here(slot, 1):
                    pe.wait_ge(cexp_ready.sem, cexp_ready.after("cexp", slot.back(1)))
                    transposed(tbank, "expT", slot, lambda c: crow[:, c * P:(c + 1) * P])
                if here(slot, 0):
                    pe.wait_ge(q_ready.sem, q_ready.after("q", slot.back(1)))
                    wbank.wait_read(pe, "kvs", slot.back(1))

                def num(fills):
                    if not here(slot, 0):
                        return
                    for k in fills:
                        b = wbank.take(pe, "num", slot, k)
                        for m in range(NUM_FILLS[k]):
                            c = sum(NUM_FILLS[:k]) + m
                            last = nc.tensor.matmul(b[:, m * NUM:(m + 1) * NUM], work_b[:, c * P:(c + 1) * P],
                                                    kv[:, slot.n % 2, :], start=True, stop=True)
                        last.then_inc(wbank.filled.sem, 1)

                num(range(RING))
                if here(slot, -2):
                    par = (slot.n - 2) // TPB % 2
                    tbank.wait_read(pe, "ln3T", slot.back(1), 3)
                    b = tbank.take(pe, "scores", slot)

                    def scores(done, blocks):
                        return split_product(nc, b[:], lambda h, c: ln3T[:, h, c, :], ctxT[par].half, blocks,
                                             stop=(blocks == DC), done=done)

                    scores(0, DC // 2)
                num(range(RING, len(NUM_FILLS)))
                if here(slot, -2):
                    scores(DC // 2, DC).then_inc(tbank.filled.sem, 1)
                if here(slot, 0):
                    wbank.wait_read(pe, "num", slot, len(NUM_FILLS) - 1)
                    transposed(wbank, "attn1", slot, lambda c: work_a[:, c, :])
                if here(slot, -1):
                    pe.wait_ge(wh_ready.sem, wh_ready.after("down", slot))
                    b = tbank.take(pe, "whT", slot)
                    nc.tensor.transpose(b[:, 0:P], wh[:], ident[:]).then_inc(tbank.filled.sem, 1)
                if here(slot, 1):
                    b1, j1 = batch(slot, 1)
                    par = (slot.n + 1) // TPB % 2
                    tbank.wait_read(pe, "expT", slot, 3)

                    def cols_split(c):
                        pe.wait_ge(t_low, c + 1)

                    if j1 == 0 and slot.n > 0:
                        pe.wait_ge(t_low, b1 * DC + DC)
                    b = wbank.take(pe, "kvs", slot)
                    split_product(nc, b[:, 0:P], lambda h, c: expT[:, h, c, :],
                                  lambda h, c: ctxT[par].half(h, c)[:, j1 * P:(j1 + 1) * P], DC,
                                  before=cols_split if slot.n < 0 else None
                                  ).then_inc(wbank.filled.sem, 1)
                if here(slot, -2):
                    tbank.wait_read(pe, "scores", slot)
                    b = tbank.take(pe, "probT", slot)
                    for m in range(TPB):
                        last = nc.tensor.transpose(b[:, m * P:(m + 1) * P], prob[:, m * P:(m + 1) * P], ident[:])
                    last.then_inc(tbank.filled.sem, 1)
                if here(slot, -1):
                    tbank.wait_read(pe, "whT", slot)
                    for k in range(NQ):
                        b = wbank.take(pe, "up", slot, k)
                        nc.tensor.matmul(b[:], whT[:], bwt_sb[:, k * Q:(k + 1) * Q], start=True, stop=True
                                         ).then_inc(wbank.filled.sem, 1)
                if here(slot, -2):
                    b2, j2 = batch(slot, -2)
                    tbank.wait_read(pe, "probT", slot)
                    for k in range(NQ):
                        if j2 == 0:
                            pe.wait_ge(n_low, b2 * DC + TPB * (k + 1))
                        b = wbank.take(pe, "pv", slot, k)
                        split_product(nc, b[:], lambda h, m: probT[:, h, m, :],
                                      lambda h, m: ctxN.half(h, TPB * k + m), TPB
                                      ).then_inc(wbank.filled.sem, 1)
                if here(slot, 0):
                    pe.wait_ge(ln2_ready.sem, ln2_ready.after("ln2", slot))
                    transposed(tbank, "ln2T", slot, lambda c: work_a[:, c, :])
                if here(slot, -1):
                    pe.wait_ge(ln3_ready.sem, ln3_ready.after("ln3", slot))
                    transposed(tbank, "ln3T", slot, lambda c: work_b[:, c * P:(c + 1) * P])

            for s in range(first, TPB):
                stages(Slot(s))
            with pe.Fori(0, (batches - 2) // 2) as r:
                for s in range(TPB, 3 * TPB):
                    stages(Slot(s, r))
            for s in range(tiles - TPB, tiles + 2):
                stages(Slot(s))


def pass_b(nc, ctx, x3, w, shared, gate_b, b_up, bias, out):
    tiles = x3.shape[0] // P
    per_round = 4
    first = -2

    def sb(name, shape, dt=F32):
        return ctx.enter_context(nc.sbuf_tensor(name, shape, dt))

    def sem(name):
        return ctx.enter_context(nc.semaphore(name))

    xt, ident, consts, scale, unscale = shared.xt, shared.ident, shared.consts, shared.scale, shared.unscale
    wt = InPlace(sb("wt", [P] + InPlace.shape((NQ - 1) * DC), F16))

    def w_half(q):
        return shared.w0.half if q == 0 else lambda h, c: wt.half(h, (q - 1) * DC + c)

    ln = sb("ln", [P, D])
    lnT = sb("lnT", [P, 2, 2, DC, P], F16)
    ag_sb = sb("ag_sb", [P, 2, DC, AG], F16)
    up1 = sb("up1", [P, D], F16)
    up2 = sb("up2", [P, D], F16)
    BIAS_HIGH, BIAS_LOW = MAXR, MAXR + 32
    stage_up = xt[:, 3, :]
    stage_bias = lnT[:, 1].rearrange("p h c a -> p (h c a)").bitcast(F32)
    order4 = sb("order4", [P, NG])
    least = sb("least", [P, MAXR])
    gb_sb = sb("gb_sb", [P, NG])
    st6 = sb("st6_b", [P, NQ, 6])
    mv = sb("mv_b", [P, 2])
    veps = sb("veps_b", [P, 1])
    rstd1 = sb("rstd1", [P, 1])
    rstd = sb("rstd_b", [P, 1])
    shift1 = sb("shift1_b", [P, 1])
    shift = sb("shift_b", [P, 1])
    fence = sb("fence_b", [P, 1])
    hs = sb("hs_b", [P, AG])
    gate = sb("gate", [P, 3, NG])
    small = sb("small", [P, 8])
    mask = sb("mask", [P, MAXR])
    hm = sb("hm", [P, 2 * MAXR])
    hmT1 = sb("hmT1", [P, P], F16)
    hmT2 = sb("hmT2", [P, P], F16)
    def counted(name, stages):
        return Counted(sem(name), stages, tiles, per_round, first)

    T_STAGES = [("hmT", 1, 0), ("lnT", 4, 1)]
    W_STAGES = [("down", 1, 0), ("main", 4, 0)]
    tbank = Banks(nc, ctx, "bt", counted("bt_filled", T_STAGES))
    wbank = Banks(nc, ctx, "bw", counted("bw_filled", W_STAGES))
    high_ready = counted("high_ready", [("hmT", 1, 0), ("lnT", 4, 1)])
    steps = counted("bsteps", [("gate", 12, 0), ("ln", NQ, 1)])
    stats_ready = counted("bstats_ready", [("ln", 1, 1)])
    pool_steps = counted("bpool_steps", [("ln", 3, 1)])
    rstd_ready = counted("brstd_ready", [("ln", 1, 1)])
    ln_ready = counted("ln_ready", [("ln", 1, 1)])
    gexp_ready = counted("gexp_ready", [("gate", 1, 0)])
    x_loaded = shared.x_loaded
    x_stored = [sem(f"bx_stored{j}") for j in range(4)]
    w_loaded = [sem(f"w_loaded{j}") for j in range(4)]
    const_loaded = sem("bconst_loaded")
    const_ready = sem("bconst_ready")
    up_blank = sem("up_blank")
    up_high = sem("up_high")
    up_low = sem("up_low")
    gb_loaded = sem("gb_loaded")
    ag_high = sem("ag_high")
    ag_low = sem("ag_low")
    high_split = sem("high_split")
    low_split = sem("low_split")

    def here(slot, offset):
        return 0 <= slot.n + offset < tiles

    def tile(slot, offset):
        return slot.n + offset + per_round * slot.rounds

    def schedule(eng, stages):
        for s in range(first, 4):
            stages(Slot(s))
        with eng.Fori(0, tiles // 4 - 2) as r:
            for s in range(4, 8):
                stages(Slot(s, r))
        for s in range(tiles - 4, tiles):
            stages(Slot(s))

    with nc.Block() as block:

        @block.sync
        def _(sp):
            for g in range((NQ - 1) * DC // 4):
                q, c = divmod(4 * g + DC, DC)
                if g >= 4:
                    sp.wait_ge(w_loaded[g % 4], 16 * (g // 4))
                sp.dma_start(wt.raw(4 * g, 4),
                             w[c * P:(c + 4) * P, q * Q:(q + 1) * Q].rearrange("(a p) n -> p a n", p=P)
                             ).then_inc(w_loaded[g % 4], 16)
                if g == 1:
                    sp.dma_start(gb_sb[:], gate_b).then_inc(gb_loaded, 16)
                if g == 3:
                    for row in (0, MAXR):
                        sp.dma_start(stage_up[row:row + MAXR, :], b_up).then_inc(const_loaded, 16)
                    for row in (BIAS_HIGH, BIAS_LOW):
                        sp.dma_start(stage_bias[row:row + 1, :], bias).then_inc(const_loaded, 16)

            def stages(slot):
                if here(slot, 2) and slot.n >= 0:
                    j = (slot.n + 2) % 4
                    if slot.n == 0 and not slot.rounds:
                        sp.wait_ge(ag_low, 1)
                    if slot.n == 1 and not slot.rounds:
                        sp.wait_ge(up_low, 1)
                    if here(slot, -2):
                        sp.wait_ge(x_stored[j], 16 * ((slot.n + 2) // 4 + slot.rounds))
                    sp.dma_start(xt[:, j, :], x3[bass.ds(tile(slot, 2) * P, P), :]).then_inc(x_loaded[j], 16)
                if here(slot, 0):
                    wbank.wait_read(sp, "main", slot, NQ - 1)
                    sp.dma_start(out[bass.ds(tile(slot, 0) * P, P), :], xt[:, slot.n % 4, :]
                                 ).then_inc(x_stored[slot.n % 4], 16)

            schedule(sp, stages)
            for j in range(4):
                sp.wait_ge(x_stored[j], 16 * (tiles // 4))

        @block.gpsimd
        def _(pool):
            for g in range(NG):
                nc.gpsimd.memset(order4[:, g:g + 1], float(NG - g))
                low = 0 if g == 0 else RANKS[g - 1]
                nc.gpsimd.memset(least[:, low:RANKS[g]], float(NG - g)).then_inc(const_ready, 1)

            def stages(slot):
                if here(slot, 1):
                    base = pool_steps.before("ln", slot)
                    pool.wait_ge(stats_ready.sem, stats_ready.after("ln", slot))
                    nc.gpsimd.tensor_tensor(shift1[:], mv[:, 0:1], consts[:, 2:3], ALU.mult)
                    nc.gpsimd.tensor_tensor(veps[:], mv[:, 1:2], consts[:, 0:1], ALU.add).then_inc(pool_steps.sem, 1)
                    pool.wait_ge(pool_steps.sem, base + 1)
                    nc.gpsimd.tensor_tensor(rstd1[:], veps[:], consts[:, 1:2], ALU.pow).then_inc(pool_steps.sem, 1)
                    pool.wait_ge(pool_steps.sem, base + 2)
                    nc.gpsimd.tensor_tensor(rstd[:], rstd1[:], consts[:, 3:4], ALU.mult).then_inc(pool_steps.sem, 1)
                    pool.wait_ge(pool_steps.sem, base + 3)
                    nc.gpsimd.tensor_tensor(shift[:], shift1[:], rstd[:], ALU.mult).then_inc(rstd_ready.sem, 1)

            schedule(pool, stages)

        @block.scalar
        def _(act):
            act.wait_ge(shared.ag_loaded, 16)
            nc.scalar.activation(ag_sb[:, 0].rearrange("p c a -> p (c a)"), xt[:, 2, 0:DC * AG], ACT.Copy,
                                 scale=scale[:, 1:2]).then_inc(ag_high, 1)

            def split_w(q):
                for c in range((q - 1) * DC, q * DC):
                    if c % 4 == 0:
                        act.wait_ge(w_loaded[c // 4 % 4], 16 * (c // 16 + 1))
                    split_high(nc, act, wt, c, scale[:, 0:1], high_split, low_split, 0)

            def stages(slot):
                if here(slot, 0):
                    act.wait_ge(steps.sem, steps.after("gate", slot, 2))
                    nc.scalar.activation(gate[:, 1, :], gate[:, 0, :], ACT.Exp, bias=small[:, 0:1],
                                         accum_out=small[:, 1:2]).then_inc(gexp_ready.sem, 1)
                once = slot.n == 0 and not slot.rounds
                if once:
                    split_w(1)
                    act.wait_ge(const_loaded, 64)
                    act.wait_ge(up_blank, 2)
                    nc.scalar.activation(up1[:], stage_up, ACT.Copy, scale=shared.up_scale[:]).then_inc(up_high, 1)
                    for row in (BIAS_HIGH, BIAS_LOW):
                        nc.scalar.activation(up2[row:row + 1, :], stage_bias[row:row + 1, :], ACT.Copy,
                                             scale=shared.bias_scale[row:row + 1, :]).then_inc(up_high, 1)
                if here(slot, 1):
                    if slot.n >= 0:
                        tbank.wait_filled(act, "lnT", slot.back(1), 3)
                    act.wait_ge(rstd_ready.sem, rstd_ready.after("ln", slot))
                    nc.scalar.activation(ln[:], xt[:, (slot.n + 1) % 4, :], ACT.Identity, scale=rstd[:], bias=shift[:]
                                         ).then_inc(ln_ready.sem, 1)
                if here(slot, 0):
                    tbank.wait_filled(act, "hmT", slot)
                    b = tbank.bank("hmT", slot)
                    nc.scalar.activation(hmT1[:], b[:, 0:P], ACT.Copy)
                    nc.scalar.activation(hmT2[0:MAXR, :], b[0:MAXR, 0:P], ACT.Copy).then_inc(high_ready.sem, 1)
                if here(slot, 1):
                    if once:
                        split_w(2)
                        split_w(3)
                        act.wait_ge(up_low, 2)
                    for k in range(4):
                        tbank.wait_filled(act, "lnT", slot, k)
                        b = tbank.bank("lnT", slot, k)
                        nc.scalar.activation(
                            lnT[:, (slot.n + 1) % 2, 0, 4 * k:4 * k + 4, :].rearrange("p a b -> p (a b)"), b[:], ACT.Copy
                        ).then_inc(high_ready.sem, 1)

            schedule(act, stages)

        @block.vector
        def _(dve):
            def split_w(q):
                for c in range((q - 1) * DC, q * DC):
                    split_low(nc, dve, wt, c, scale[:, 0:1], high_split, low_split, 0)

            def main(slot, k):
                part = xt[:, slot.n % 4, k * Q:(k + 1) * Q]
                wbank.wait_filled(dve, "main", slot, k)
                nc.vector.scalar_tensor_tensor(part, wbank.bank("main", slot, k)[:], unscale[:, 0:1], part, ALU.mult,
                                               ALU.add).then_inc(wbank.sem("main", slot, k), 1)

            def stages(slot):
                once = slot.n == 0 and not slot.rounds
                if once:
                    dve.wait_ge(gb_loaded, 16)
                    dve.wait_ge(const_ready, NG)
                if here(slot, 0):
                    base = steps.before("gate", slot)
                    done = 0

                    def step(ins):
                        nonlocal done
                        done += 1
                        ins.then_inc(steps.sem, 1)
                        dve.wait_ge(steps.sem, base + done)

                    wbank.wait_filled(dve, "down", slot)
                    nc.vector.tensor_scalar(hs[:], wbank.bank("down", slot)[:, 0:AG], unscale[:, 1:2], None, ALU.mult
                                            ).then_inc(wbank.sem("down", slot), 1)
                    wbank.wait_read(dve, "down", slot)
                    step(nc.vector.tensor_tensor(gate[:, 0, :], hs[:, MAXR:], gb_sb[:], ALU.add))
                    step(nc.vector.tensor_reduce(small[:, 0:1], gate[:, 0, :], AX_X, ALU.max, negate=True))
                    dve.wait_ge(gexp_ready.sem, gexp_ready.after("gate", slot))
                    step(nc.vector.reciprocal(small[:, 2:3], small[:, 1:2]))
                    step(nc.vector.tensor_scalar(gate[:, 0, :], gate[:, 1, :], small[:, 2:3], None, ALU.mult))
                    step(nc.vector.tensor_reduce(small[:, 3:4], gate[:, 0, :], AX_X, ALU.max))
                    step(nc.vector.scalar_tensor_tensor(gate[:, 2, :], gate[:, 0, :], small[:, 3:4], order4[:],
                                                        ALU.is_equal, ALU.mult))
                    step(nc.vector.reciprocal(small[:, 4:5], small[:, 3:4]))
                    step(nc.vector.tensor_tensor(small[:, 5:6], small[:, 3:4], small[:, 4:5], ALU.mult))
                    step(nc.vector.tensor_reduce(small[:, 6:7], gate[:, 2, :], AX_X, ALU.max))
                    step(nc.vector.tensor_scalar(mask[:], least[:], small[:, 6:7], small[:, 5:6], ALU.is_ge, ALU.mult))
                    step(nc.vector.tensor_scalar(hs[:, 0:MAXR], hs[:, 0:MAXR], shared.h_scale[:], None, ALU.mult))
                    step(nc.vector.tensor_tensor(hm[:].rearrange("p (h r) -> p h r", h=2),
                                                 hs[:, 0:MAXR].unsqueeze(1).broadcast_to([P, 2, MAXR]),
                                                 mask[:].unsqueeze(1).broadcast_to([P, 2, MAXR]), ALU.mult))
                if here(slot, 1):
                    j1 = (slot.n + 1) % 4
                    base = steps.before("ln", slot)
                    dve.wait_ge(x_loaded[j1], 16 * ((slot.n + 1) // 4 + slot.rounds) + 16)
                    for k in range(NQ):
                        nc.vector.bn_stats(st6[:, k, :], xt[:, j1, k * Q:(k + 1) * Q]).then_inc(steps.sem, 1)
                    dve.wait_ge(steps.sem, base + NQ)
                    nc.vector.memset(fence[:], 0.0)
                    nc.vector.bn_aggr(mv[:], st6[:]).then_inc(stats_ready.sem, 1)
                if slot.n == -1:
                    nc.vector.memset(up2[MAXR:P, :], 0.0).then_inc(up_blank, 1)
                    nc.vector.memset(hmT2[MAXR:P, :], 0.0).then_inc(up_blank, 1)
                    dve.wait_ge(up_blank, 2)
                    for row in (BIAS_HIGH, BIAS_LOW):
                        nc.vector.memset(hmT2[row:row + 1, :], BIAS_ROW).then_inc(up_blank, 1)
                    dve.wait_ge(ag_high, 1)
                    nc.vector.scalar_tensor_tensor(ag_sb[:, 1].rearrange("p c a -> p (c a)"), xt[:, 2, 0:DC * AG],
                                                   scale[:, 1:2], ag_sb[:, 0].rearrange("p c a -> p (c a)"),
                                                   ALU.mult, ALU.subtract).then_inc(ag_low, 1)
                if once:
                    split_w(1)
                    dve.wait_ge(up_high, 1)
                    nc.vector.scalar_tensor_tensor(up2[0:MAXR, :], stage_up[0:MAXR, :], shared.up_scale[0:MAXR, :],
                                                   up1[0:MAXR, :], ALU.mult, ALU.subtract).then_inc(up_low, 1)
                    dve.wait_ge(up_high, 3)
                    row = slice(BIAS_LOW, BIAS_LOW + 1)
                    nc.vector.scalar_tensor_tensor(up2[row, :], stage_bias[row, :], shared.bias_scale[row, :],
                                                   up2[row, :], ALU.mult, ALU.subtract).then_inc(up_low, 1)
                if here(slot, 0):
                    dve.wait_ge(high_ready.sem, high_ready.after("hmT", slot))
                    nc.vector.tensor_tensor(hmT1[MAXR:P, :], tbank.bank("hmT", slot)[MAXR:P, 0:P], hmT1[MAXR:P, :],
                                            ALU.subtract).then_inc(tbank.sem("hmT", slot), 1)
                    if once:
                        split_w(2)
                    main(slot, 0)
                    main(slot, 1)
                    if once:
                        split_w(3)
                    main(slot, 2)
                if here(slot, 1):
                    for k in range(4):
                        dve.wait_ge(high_ready.sem, high_ready.after("lnT", slot, k + 1))
                        two = [lnT[:, (slot.n + 1) % 2, h, 4 * k:4 * k + 4, :].rearrange("p a b -> p (a b)")
                               for h in range(2)]
                        nc.vector.tensor_tensor(two[1], tbank.bank("lnT", slot, k)[:], two[0], ALU.subtract
                                                ).then_inc(tbank.sem("lnT", slot, k), 1)
                if here(slot, 0):
                    main(slot, 3)

            schedule(dve, stages)

        @block.tensor
        def _(pe):
            def main(slot, k):
                def split_ready(c):
                    if c % 4 == 0:
                        pe.wait_ge(low_split, (k - 1) * DC + c + 4)

                b = wbank.take(pe, "main", slot, k)
                split_product(nc, b[:], lambda h, c: lnT[:, slot.n % 2, h, c, :], w_half(k), DC, stop=False,
                              before=split_ready if slot.n == 0 and not slot.rounds and k > 0 else None)
                return b

            def lora_up(b, k):
                nc.tensor.matmul(b[:], hmT1[:], up1[:, k * Q:(k + 1) * Q], start=False, stop=False)
                nc.tensor.matmul(b[:], hmT2[:], up2[:, k * Q:(k + 1) * Q], start=False, stop=True
                                 ).then_inc(wbank.filled.sem, 1)

            def stages(slot):
                if here(slot, 0):
                    tbank.wait_read(pe, "lnT", slot.back(1), 3)
                    if slot.n == 0 and not slot.rounds:
                        pe.wait_ge(ag_low, 1)
                    b = wbank.take(pe, "down", slot)
                    split_product(nc, b[:, 0:AG], lambda h, c: lnT[:, slot.n % 2, h, c, :],
                                  lambda h, c: ag_sb[:, h, c, :], DC).then_inc(wbank.filled.sem, 1)
                    b0 = main(slot, 0)
                    pe.wait_ge(steps.sem, steps.after("gate", slot))
                    t = tbank.take(pe, "hmT", slot)
                    nc.tensor.transpose(t[:, 0:P], hm[:], ident[:]).then_inc(tbank.filled.sem, 1)
                    b1 = main(slot, 1)
                    tbank.wait_read(pe, "hmT", slot)
                    if slot.n == 0 and not slot.rounds:
                        pe.wait_ge(up_low, 2)
                        pe.wait_ge(up_blank, 4)
                    lora_up(b0, 0)
                    lora_up(b1, 1)
                    lora_up(main(slot, 2), 2)
                if here(slot, 1):
                    pe.wait_ge(ln_ready.sem, ln_ready.after("ln", slot))
                    for k in range(4):
                        b = tbank.take(pe, "lnT", slot, k)
                        for m in range(4):
                            c = 4 * k + m
                            last = nc.tensor.transpose(b[:, m * P:(m + 1) * P], ln[:, c * P:(c + 1) * P], ident[:])
                        last.then_inc(tbank.filled.sem, 1)
                if here(slot, 0):
                    lora_up(main(slot, 3), 3)

            schedule(pe, stages)


def program(nc, x, c_rows, c_cols, ra, bwt, w, ag, gate_b, b_up, bias, out):
    x3 = nc.dram_tensor("x3", x.shape, F32, kind="Internal").ap()
    tiles = x.shape[0] // P
    with ExitStack() as both:
        shared = Shared(nc, both, tiles)
        with ExitStack() as ctx:
            pass_a(nc, ctx, x, c_rows, c_cols, ra, bwt, w, ag, b_up, bias, shared, x3)
        with ExitStack() as ctx:
            pass_b(nc, ctx, x3, w, shared, gate_b, b_up, bias, out)


def kernel(x, ctx_4096, L0_ffn_route_w, L0_ffn_A, L0_ffn_Bw, L1_ffn_W, L1_ffn_b, L1_ffn_A, L1_ffn_B,
           L1_ffn_gate_w, L1_ffn_gate_b):
    import numpy as np
    from concourse import bacc
    from concourse.bass_utils import run_bass_kernel_spmd

    shape = x.shape
    batches = shape[0]
    rows = batches * ROWS
    c = np.asarray(ctx_4096)

    def blocks(a):
        return np.ascontiguousarray(a.T.reshape(DC, P, a.shape[0]).transpose(1, 0, 2))

    arrays = {
        "x": np.ascontiguousarray(np.asarray(x).reshape(rows, D)),
        "c_rows": np.ascontiguousarray(c.reshape(rows, D)),
        "c_cols": np.ascontiguousarray(c.reshape(batches, ROWS, DC, P).transpose(0, 3, 2, 1).reshape(batches * P, DC, ROWS)),
        "ra": blocks(np.concatenate([np.asarray(L0_ffn_route_w), np.asarray(L0_ffn_A).reshape(ER, D)])),
        "bwt": np.ascontiguousarray(np.asarray(L0_ffn_Bw).transpose(0, 2, 1).reshape(ER, D)),
        "w": np.ascontiguousarray(np.asarray(L1_ffn_W).T),
        "ag": blocks(np.concatenate([np.asarray(L1_ffn_A), np.asarray(L1_ffn_gate_w)])),
        "gate_b": np.ascontiguousarray(np.broadcast_to(np.asarray(L1_ffn_gate_b), (P, NG))),
        "b_up": np.ascontiguousarray(np.asarray(L1_ffn_B).T),
        "bias": np.ascontiguousarray(np.asarray(L1_ffn_b).reshape(1, D)),
    }
    nc = bacc.Bacc("TRN2", target_bir_lowering=False, num_devices=1)
    aps = {n: nc.dram_tensor(n, a.shape, F32, kind="ExternalInput").ap() for n, a in arrays.items()}
    out = nc.dram_tensor("out", (rows, D), F32, kind="ExternalOutput").ap()
    program(nc, **aps, out=out)
    result = run_bass_kernel_spmd(nc, [arrays], core_ids=[0])
    return result.results[0]["out"].reshape(shape)
```
